# Optimizing a Trainium2 kernel written in Bass

```python
import numpy as np
import jax
import jax.numpy as jnp

def _softmax(x, axis=-1):
    return jax.nn.softmax(x, axis=axis)
def _gelu(x):
    return jax.nn.gelu(x, approximate=True)
def _silu(x):
    return jax.nn.silu(x)
def _sigmoid(x):
    return jax.nn.sigmoid(x)
def _layernorm(x, axis=-1, eps=1e-5):
    m = jnp.mean(x, axis=axis, keepdims=True)
    v = jnp.var(x, axis=axis, keepdims=True)
    return (x - m) / jnp.sqrt(v + eps)
def _scatter_add(tgt, idx, src, axis=0):
    return tgt.at[idx].add(src)
def _segment_sum(src, seg, n):
    return jax.ops.segment_sum(src, seg, n)

kernel_name = 'mk_adj_resnorm_d1_adj_256_496fc5'

def setup_inputs(seed: int = 0):
    np.random.seed(seed)
    _w = jnp.asarray
    def _rec_inputs():
        import jax
        import jax.numpy as jnp
        _gk = jax.random.key(seed)
        x = -0.0005146 + 1 * jax.random.normal(jax.random.fold_in(_gk, 1), (8, 2048, 256), jnp.float32)
        _a = jax.random.bernoulli(jax.random.fold_in(_gk, 2), 0.00390625, (8, 2048, 2048))
        adj = _a.astype(jnp.int32)
        return x, adj
    x, adj = _rec_inputs()
    def _L0_gnn_setup():
        import jax, jax.numpy as jnp
        import numpy as np
        B, N, C, OUT, S = (4, 2048, 256, 256, 25)
        DENSITY = 0.008
        key = jax.random.key(seed)
        kA, kX, kW = jax.random.split(key, 3)
        A = jax.random.bernoulli(kA, DENSITY, (B, N, N)).astype(jnp.int32)
        X = jax.random.normal(kX, (B, N, C), dtype=jnp.float32)
        W = jax.random.normal(kW, (2 * C, OUT), dtype=jnp.float32) * np.float32(1.0 / np.sqrt(2 * C))
        b = jnp.zeros((OUT,), dtype=jnp.float32)
        return {'A': A, 'X': X, 'W': W, 'b': b}
    _L0_gnn_all = _L0_gnn_setup()
    _L0_gnn_in = {k: v for k, v in _L0_gnn_all.items() if k in ('W', 'b', )}
    del _L0_gnn_all

    return {
        "x": x,
        "adj": adj,
        "L0_gnn_W": _L0_gnn_in["W"],
        "L0_gnn_b": _L0_gnn_in["b"],
    }

def reference(x, adj, L0_gnn_W, L0_gnn_b):
    import jax
    import jax.numpy as jnp
    def _L0_gnn_ref(A, X, W, b):
        import jax, jax.numpy as jnp
        import numpy as np
        B, N, C, OUT, S = (4, 2048, 256, 256, 25)
        DENSITY = 0.008
        mask = A != 0
        neg_inf = jnp.float32(-jnp.inf)
        pri = -jnp.arange(N, dtype=jnp.float32)
        scores = jnp.where(mask, pri, neg_inf)
        vals, idx = jax.lax.top_k(scores, S)
        valid = vals > neg_inf
        feats = jax.vmap(lambda x, i: x[i])(X, idx)
        feats = jnp.where(valid[..., None], feats, neg_inf)
        agg = feats.max(axis=2)
        degree = mask.sum(axis=-1)
        agg = jnp.where((degree <= S)[..., None], jnp.maximum(agg, 0.0), agg)
        h = jnp.concatenate([X, agg], axis=-1)
        out = jax.nn.relu(jnp.einsum('bnf,fo->bno', h, W) + b)
        return out

    x = _layernorm(x + _L0_gnn_ref(adj, x, L0_gnn_W, L0_gnn_b), axis=-1)
    return x


_drawn_inputs = setup_inputs


def setup_inputs(seed=0):
    import zlib

    import numpy as np

    out = dict(_drawn_inputs(seed))
    spreads = {'L0_gnn_b': (0.0, 0.1)}
    factors = {}
    for name, (base, spread) in spreads.items():
        noise = np.random.default_rng([zlib.crc32(name.encode()), seed]).standard_normal(out[name].shape)
        drawn = base * np.exp(spread * noise) if base else spread * noise
        out[name] = jnp.asarray(drawn.astype(out[name].dtype))
    for name, factor in factors.items():
        out[name] = (out[name] * factor).astype(out[name].dtype)
    return out
```

```python
from contextlib import ExitStack

import concourse.bass as bass
from concourse import mybir

F32 = mybir.dt.float32
F16 = mybir.dt.float16
BF16 = mybir.dt.bfloat16
I32 = mybir.dt.int32
U32 = mybir.dt.uint32
ALU = mybir.AluOpType
ACT = mybir.ActivationFunctionType
AX = mybir.AxisListType

P = 128
S = 25
TOP = 32
CH = 256
TG = 8
G = TG * P
HB = TG // 2
RLAG = TG + 3
FLAG = 2 * TG + 3
NGB = 4
NMB = 2
MAIN = 12
OVF = S - MAIN
BASE = 4
DCAP = S + 1
NC = DCAP + 1
SKIP = float(1 << 20)
LOWEST = -3.4028235e38
EPS = 1e-5
CLASSES = [4, 5, 6, 7, 8, 9, 10, 11, 12]


def build(nc, x, adj, W, b, out):
    NB, N, C = x.shape
    OUT = W.shape[1]
    NG = NB * N // G
    NCH = N // CH
    KC = C // P
    assert N == 2048 and N % G == 0 and C == OUT == 256 and G % 512 == 0 and NG > 4

    adj_v = adj.rearrange("b n m -> (b n) m").rearrange("(g p t) m -> g t p m", p=P, t=TG)
    x_rows = x.rearrange("b n c -> (b n) c")
    x_v = x_rows.rearrange("(g p h t) c -> g h p t c", p=P, h=2, t=HB)
    out_v = out.rearrange("b n c -> (b n) c").rearrange("(g p h t) c -> g h p t c", p=P, h=2, t=HB)
    W_v = W.rearrange("(k p) n -> p k n", p=P)

    with ExitStack() as ctx:
        def sb(name, shape, dt):
            return ctx.enter_context(nc.sbuf_tensor(name, shape, dt))

        def psum(name, shape, dt):
            return ctx.enter_context(nc.psum_tensor(name, shape, dt))

        def sem(name):
            return ctx.enter_context(nc.semaphore(name))

        score_of = sb("score_of", [P, N], F16)
        column_of = sb("column_of", [P, G], F16)
        place_of = sb("place_of", [P, TG], F32)
        class_deg = sb("class_deg", [P, NC], F16)
        table_end = sb("table_end", [P, NG], F32)
        ones = sb("ones", [P, P], F16)
        ident = sb("ident", [P, P], F16)
        before = sb("before", [P, P], F16)
        onesf = sb("onesf", [P, P], F32)
        identf = sb("identf", [P, P], F32)
        zeros = sb("zeros", [P, 1], F32)
        eps = sb("eps", [P, 1], F32)
        w_sb = sb("w_sb", [P, 2 * KC, OUT], F32)
        b_sb = sb("b_sb", [1, OUT], F32)
        adj_sb = sb("adj_sb", [P, NMB, N], I32)
        mask = sb("mask", [P, NMB, N], F16)
        score = sb("score", [P, TG, N], F16)
        cand = sb("cand", [P, TG, NCH, 8], F16)
        rest = sb("rest", [P, 2, NCH * 8], F16)
        top = sb("top", [P, TG, TOP], F16)
        crowded = sb("crowded", [P, 1], F16)
        crowded_i = sb("crowded_i", [1, 1], I32)
        found = sb("found", [P, TG, TOP], F16)
        deg = sb("deg", [P, TG], F32)
        inclass = sb("inclass", [P, TG, NC], F16)
        above = sb("above", [P, TG, NC], F16)
        above_sum = sb("above_sum", [P, NC], F16)
        picked = sb("picked", [P, TG, NC], F32)
        pos = sb("pos", [P, TG], F32)
        to_sorted = sb("to_sorted", [P, TG, G], F16)
        missing = sb("missing", [P, TG, S], F32)
        minus = sb("minus", [P, TG, S], F32)
        lists = sb("lists", [P, TG, S + 1], I32)
        floor = sb("floor", [P, TG], F32)
        posdiag = sb("posdiag", [P, TG, P], F16)
        posrow = sb("posrow", [P, G], F16)
        from_sorted = sb("from_sorted", [P, 2, G], BF16)
        nbr = [sb(f"nbr{i}", [P, MAIN, C], F32) for i in range(NGB)]
        over = [sb(f"over{i}", [P, OVF, C], F32) for i in range(2)]
        agg = sb("agg", [P, 2, C], F32)
        agg_over = sb("agg_over", [P, C], F32)
        part = sb("part", [P, 2, 3, C], BF16)
        resid = sb("resid", [P, C], F32)
        aggT = sb("aggT", [P, KC, G], F32)
        x_sb = [sb(f"x_sb{h}", [P, HB, C], F32) for h in range(2)]
        xT = sb("xT", [P, KC, P], F32)
        z = sb("z", [P, 2, OUT], F32)
        stats = sb("stats", [P, 6], F32)
        meanvar = sb("meanvar", [P, 2, 2], F32)
        sd = sb("sd", [P, 2, 1], F32)
        rstd = sb("rstd", [P, 1], F32)
        y_sb = [sb(f"y_sb{h}", [P, HB, OUT], F32) for h in range(2)]

        ps_agg = psum("ps_agg", [P, KC, G], F32)
        ps_y = psum("ps_y", [P, 512], F32)
        ps_xT = psum("ps_xT", [P, 512], F32)
        ps_rank = psum("ps_rank", [P, 512], F32)
        ps_pos = psum("ps_pos", [P, 512], F32)
        xT_ps = ps_xT[:, 0:C].rearrange("p (k m) -> p k m", k=KC)
        crowd_ps = ps_xT[0:1, C:C + 1]
        place_ps = ps_rank[:, 0:TG * NC].rearrange("p (t c) -> p t c", t=TG)
        list_ps = ps_rank[:, 0:TG * (S + 1)].rearrange("p (t s) -> p t s", t=TG)

        s_const = sem("s_const")
        s_ident = sem("s_ident")
        s_w = sem("s_w")
        s_adj = [sem(f"s_adj{i}") for i in range(NMB)]
        s_x = [sem(f"s_x{h}") for h in range(2)]
        s_store = [sem(f"s_store{h}") for h in range(2)]
        s_mask = sem("s_mask")
        s_zero = sem("s_zero")
        s_aggT = sem("s_aggT")
        s_xT = sem("s_xT")
        s_sd = sem("s_sd")
        s_posrow = sem("s_posrow")
        s_score = sem("s_score")
        s_cand = sem("s_cand")
        s_top = sem("s_top")
        s_rest = sem("s_rest")
        s_crowd = sem("s_crowd")
        s_crowd_i = sem("s_crowd_i")
        s_redo = sem("s_redo")
        s_deg = sem("s_deg")
        s_class = sem("s_class")
        s_pos = sem("s_pos")
        s_perm = sem("s_perm")
        s_list = sem("s_list")
        s_diag = sem("s_diag")
        s_back = sem("s_back")
        s_max = sem("s_max")
        s_over = sem("s_over")
        s_part = sem("s_part")
        s_z = sem("s_z")
        s_stats = sem("s_stats")
        s_mv = sem("s_mv")
        s_rstd = sem("s_rstd")
        s_y = sem("s_y")
        s_crowd_mm = sem("s_crowd_mm")
        s_rank_mm = sem("s_rank_mm")
        s_list_mm = sem("s_list_mm")
        s_pos_mm = sem("s_pos_mm")
        s_back_mm = sem("s_back_mm")
        s_xT_mm = sem("s_xT_mm")
        s_y_mm = sem("s_y_mm")
        s_gather = [sem(f"s_gather{i}") for i in range(NGB)]
        s_skip = [sem(f"s_over_in{i}") for i in range(2)]
        NH = G // 512
        REDO = 7 * TG
        PARTA = TG - 3

        def wait(eng, s, value):
            if not isinstance(value, int) or value > 0:
                eng.wait_ge(s, value)

        def hold(eng, s, value):
            if not isinstance(value, int):
                value = eng.to_reg(value)
            eng.wait_ge(s_const, 2)
            wait(eng, s, value)

        def live(g):
            return not isinstance(g, int) or 0 <= g < NG

        def lagged(k, i, lag):
            d, t = divmod(i - lag, TG)
            return k + d, t

        def run(eng, body):
            for k in range(3):
                body(k)
            with eng.Fori(3, NG) as k:
                body(k)
            for k in range(NG, NG + 3):
                body(k)

        block = ctx.enter_context(nc.Block())

        @block.sync
        def _(sp):
            sp.dma_start(w_sb[:], W_v).then_inc(s_w, 16)
            sp.dma_start(b_sb[:], b.rearrange("(a n) -> a n", a=1)).then_inc(s_w, 16)

            def load_adj(g):
                for t in range(TG):
                    wait(sp, s_mask, g * TG + t + 1 - NMB)
                    sp.dma_start(adj_sb[:, t % NMB, :], adj_v[g, t]).then_inc(s_adj[t % NMB], 16)

            load_adj(0)
            with sp.Fori(1, NG) as g:
                load_adj(g)

        @block.gpsimd
        def _(pool):
            pool.iota(score_of[:], [[-1, N]], base=N, channel_multiplier=0,
                      allow_small_or_imprecise_dtypes=True)
            pool.iota(column_of[:], [[1, G]], base=0, channel_multiplier=0,
                      allow_small_or_imprecise_dtypes=True)
            pool.iota(place_of[:], [[P, TG]], base=0, channel_multiplier=1,
                      allow_small_or_imprecise_dtypes=True)
            pool.iota(class_deg[:], [[-1, NC]], base=DCAP, channel_multiplier=0,
                      allow_small_or_imprecise_dtypes=True)
            pool.iota(table_end[:], [[N, NB], [0, NG // NB]], base=N, channel_multiplier=0,
                      allow_small_or_imprecise_dtypes=True)
            pool.memset(zeros[:], 0.0)
            pool.memset(eps[:], EPS)
            pool.memset(onesf[:], 1.0)
            pool.memset(over[0][:], 0.0)
            pool.memset(over[1][:], 0.0)
            pool.memset(ones[:], 1.0).then_inc(s_const, 1)
            pool.wait_ge(s_const, 1)
            pool.affine_select(out=ident[:], in_=ones[:], compare_op=ALU.is_equal, fill=0.0, base=0,
                               pattern=[[-1, P]], channel_multiplier=1)
            pool.affine_select(out=before[:], in_=ones[:], compare_op=ALU.is_gt, fill=0.0, base=0,
                               pattern=[[1, P]], channel_multiplier=-1).then_inc(s_const, 1)

            def gather(dst, t, slot, s):
                pool.indirect_dma_start(
                    out=dst, out_offset=None, in_=x_rows,
                    in_offset=bass.IndirectOffsetOnAxis(ap=lists[:, t, slot:slot + 1], axis=0),
                    bounds_check=NB * N - 1, oob_is_err=False).then_inc(s, 16)

            def main_slots(t, slot, degree):
                if slot == MAIN:
                    return
                with pool.If(degree > slot):
                    gather(nbr[t % NGB][:, slot, :], t, slot, s_gather[t % NGB])
                    main_slots(t, slot + 1, degree)
                with pool.Else():
                    pool.inc_swdge_sem([s_gather[t % NGB]], [16 * (MAIN - slot)])

            def over_slots(t, slot, degree):
                o = over[t > 0]
                s = s_skip[t > 0]
                end = slot + 4 if slot + 8 <= S else S
                for j in range(slot, end):
                    gather(o[:, j - MAIN, :], t, j, s)
                if end < S:
                    with pool.If(degree > end):
                        over_slots(t, end, degree)
                    with pool.Else():
                        pool.inc_swdge_sem([s], [16 * (S - end)])

            def gathers(g):
                for t in range(TG):
                    if t in (0, PARTA):
                        hold(pool, s_list, 3 * (2 * g + 1 + (t >= PARTA)))
                    degree = pool.value_load(lists[0:1, t, S:S + 1], min_val=0, max_val=DCAP)
                    hold(pool, s_zero, g * TG + t + 1)
                    for slot in range(BASE):
                        gather(nbr[t % NGB][:, slot, :], t, slot, s_gather[t % NGB])
                    main_slots(t, BASE, degree)
                    with pool.If(degree > MAIN):
                        if t == 0:
                            hold(pool, s_over, 3 * ((g - 1) * TG + 1))
                        elif t == 1:
                            hold(pool, s_over, 3 * g * TG)
                        else:
                            hold(pool, s_over, 3 * (g * TG + t))
                        over_slots(t, MAIN, degree)
                        if t:
                            hold(pool, s_skip[1], 16 * OVF * (g * (TG - 1) + t))
                    with pool.Else():
                        pool.inc_swdge_sem([s_skip[t > 0]], [16 * OVF])

            gathers(0)
            with pool.Fori(1, NG) as g:
                gathers(g)

        @block.scalar
        def _(act):
            act.wait_ge(s_const, 1)
            act.activation(sd[:, 0, :], eps[:], ACT.Sqrt).then_inc(s_sd, 1)

            def load_x(g, h, used):
                wait(act, s_z, used)
                act.dma_start(x_sb[h][:], x_v[g, h]).then_inc(s_x[h], 16)

            def store_y(g, h):
                act.wait_ge(s_y, g * TG + HB * (h + 1))
                act.dma_start(out_v[g, h], y_sb[h][:]).then_inc(s_store[h], 16)

            def copy_posrow(g, n):
                act.wait_ge(s_pos_mm, g * NH + n + 1)
                if n == 0:
                    wait(act, s_back, g * TG)
                act.activation(posrow[:, n * 512:(n + 1) * 512], ps_pos[:], ACT.Copy).then_inc(s_posrow, 1)

            def body(k):
                for i in range(TG):
                    fg, ft = lagged(k, i, FLAG)
                    rg, rt = lagged(k, i, RLAG)
                    if i == 0:
                        if live(k - 3):
                            store_y(k - 3, 0)
                        if live(k - 2):
                            load_x(k - 2, 0, (k - 3) * TG + HB)
                    if i == 3:
                        if live(k - 1):
                            for n in range(1, NH):
                                copy_posrow(k - 1, n)
                        if live(k - 2):
                            act.wait_ge(s_back_mm, (k - 1) * TG)
                            wait(act, s_y_mm, (k - 2) * TG)
                            for c in range(KC):
                                act.activation(aggT[:, c, :], ps_agg[:, c, :], ACT.Copy).then_inc(s_aggT, 1)
                            load_x(k - 2, 1, (k - 2) * TG)
                    if i == 4 and live(k - 3):
                        store_y(k - 3, 1)
                    if live(fg):
                        u = fg * TG + ft
                        act.wait_ge(s_xT_mm, u + 1)
                        wait(act, s_y_mm, u)
                        act.activation(xT[:], xT_ps, ACT.Copy).then_inc(s_xT, 1)
                    if live(k):
                        u = k * TG + i
                        act.wait_ge(s_adj[i % NMB], 16 * (k * (TG // NMB) + i // NMB + 1))
                        wait(act, s_score, u + 1 - NMB)
                        act.activation(mask[:, i % NMB, :], adj_sb[:, i % NMB, :].bitcast(U32),
                                       ACT.Sign).then_inc(s_mask, 1)
                    if i == 2 and live(k - 1):
                        copy_posrow(k - 1, 0)
                    zg, zt = lagged(k, i, RLAG - NGB)
                    if live(zg):
                        wait(act, s_max, zg * TG + zt + 1 - NGB)
                        act.activation(nbr[zt % NGB][:], zeros[:].unsqueeze(2).to_broadcast([P, MAIN, C]),
                                       ACT.Copy).then_inc(s_zero, 1)
                    if live(fg):
                        u = fg * TG + ft
                        act.wait_ge(s_mv, u + 1)
                        wait(act, s_rstd, u - 1)
                        act.activation(sd[:, ft % 2, :], meanvar[:, ft % 2, 1:2], ACT.Sqrt,
                                       bias=eps[:]).then_inc(s_sd, 1)

            act.wait_ge(s_sd, 1)
            run(act, body)
            for h in range(2):
                act.wait_ge(s_store[h], 16 * NG)

        @block.tensor
        def _(pe):
            pe.wait_ge(s_const, 2)
            pe.wait_ge(s_ident, 1)
            pe.wait_ge(s_w, 32)

            def pos_rows(g, n):
                pe.wait_ge(s_diag, g + 1)
                wait(pe, s_posrow, g * NH + n)
                pe.matmul(ps_pos[:], ones[:], posdiag[:, 4 * n:4 * n + 4, :],
                          start=True, stop=True).then_inc(s_pos_mm, 1)

            def body(k):
                for i in range(TG):
                    fg, ft = lagged(k, i, FLAG)
                    rg, rt = lagged(k, i, RLAG)
                    if i == 3 and live(k - 1):
                        for n in range(1, NH):
                            pos_rows(k - 1, n)
                    if live(fg):
                        u = fg * TG + ft
                        pe.wait_ge(s_x[ft // HB], 16 * (fg + 1))
                        wait(pe, s_xT, u)
                        if i == 0 and live(k - 1):
                            pe.wait_ge(s_crowd_i, k)
                        for c in range(KC):
                            mm = pe.transpose(xT_ps[:, c, :], x_sb[ft // HB][:, ft % HB, c * P:(c + 1) * P], identf[:])
                        mm.then_inc(s_xT_mm, 1)
                    if i == 2 and live(k - 1):
                        pos_rows(k - 1, 0)
                    if live(rg):
                        u = rg * TG + rt
                        if rt == 0:
                            wait(pe, s_aggT, KC * rg)
                        pe.wait_ge(s_part, 4 * (u + 1))
                        for c in range(KC):
                            for n in range(NH):
                                for q in range(3):
                                    mm = pe.matmul(ps_agg[:, c, n * 512:(n + 1) * 512],
                                                   part[:, rt % 2, q, c * P:(c + 1) * P],
                                                   from_sorted[:, rt % 2, n * 512:(n + 1) * 512],
                                                   start=(rt == 0 and q == 0), stop=(rt == TG - 1 and q == 2))
                        mm.then_inc(s_back_mm, 1)
                    if live(fg):
                        u = fg * TG + ft
                        wait(pe, s_z, u)
                        y = ps_y[:, 0:OUT]
                        pe.matmul(y, onesf[0:1, :], b_sb[:], start=True, stop=False)
                        if ft == 0:
                            pe.wait_ge(s_aggT, KC * (fg + 1))
                        for c in range(KC):
                            pe.matmul(y, aggT[:, c, ft * P:(ft + 1) * P], w_sb[:, KC + c, :], start=False, stop=False)
                        pe.wait_ge(s_xT, u + 1)
                        for c in range(KC):
                            mm = pe.matmul(y, xT[:, c, :], w_sb[:, c, :], start=False, stop=(c == KC - 1))
                        mm.then_inc(s_y_mm, 1)
                if live(k):
                    pe.wait_ge(s_crowd, k + 1)
                    wait(pe, s_xT, (k - 2) * TG + TG - FLAG % TG)
                    pe.matmul(crowd_ps, crowded[:], ones[:, 0:1], start=True, stop=True).then_inc(s_crowd_mm, 1)
                    pe.wait_ge(s_class, 3 * (k + 1))
                    wait(pe, s_list, 3 * 2 * k)
                    for t in range(TG):
                        pe.matmul(place_ps[:, t, :], before[:], inclass[:, t, :], start=True, stop=False)
                        for e in range(t):
                            pe.matmul(place_ps[:, t, :], ones[:], inclass[:, e, :], start=False, stop=False)
                        mm = pe.matmul(place_ps[:, t, :], ones[:], above_sum[:], start=False, stop=True)
                    mm.then_inc(s_rank_mm, 1)
                    pe.wait_ge(s_perm, k + 1)
                    for o in range(TG):
                        for t in range(TG):
                            mm = pe.matmul(list_ps[:, o, :], to_sorted[:, t, o * P:(o + 1) * P],
                                           top[:, t, 0:S + 1], start=(t == 0), stop=(t == TG - 1))
                    mm.then_inc(s_list_mm, 1)

            run(pe, body)

        @block.vector
        def _(dve):
            dve.wait_ge(s_const, 2)
            dve.tensor_copy(identf[:], ident[:]).then_inc(s_ident, 1)

            def extract(g, t):
                u = g * TG + t
                dve.wait_ge(s_mask, u + 1)
                dve.tensor_tensor(score[:, t, :], mask[:, t % NMB, :], score_of[:], ALU.mult).then_inc(s_score, 1)
                hold(dve, s_score, u + 1)
                for c in range(NCH):
                    ins = dve.max(cand[:, t, c, :], score[:, t, c * CH:(c + 1) * CH])
                ins.then_inc(s_cand, 1)
                hold(dve, s_cand, u + 1)
                src = cand[:, t].rearrange("p c e -> p (c e)")
                for r in range(TOP // 8):
                    best = top[:, t, 8 * r:8 * r + 8]
                    dve.max(best, src).then_inc(s_top, 1)
                    hold(dve, s_top, 4 * u + r + 1)
                    if r < TOP // 8 - 1:
                        dve.match_replace(rest[:, r % 2, :], best, src, 0.0).then_inc(s_rest, 1)
                        hold(dve, s_rest, 3 * u + r + 1)
                        src = rest[:, r % 2, :]

            def extract_again(g):
                n = 0
                for t in range(TG):
                    src = score[:, t, :]
                    for r in range(TOP // 8):
                        best = top[:, t, 8 * r:8 * r + 8]
                        dve.max(best, src).then_inc(s_redo, 1)
                        n += 1
                        hold(dve, s_redo, g * REDO + n)
                        if r < TOP // 8 - 1:
                            left = to_sorted[:, 2 * (r % 2):2 * (r % 2) + 2, :].rearrange("p a n -> p (a n)")
                            dve.match_replace(left, best, src, 0.0).then_inc(s_redo, 1)
                            n += 1
                            hold(dve, s_redo, g * REDO + n)
                            src = left
                assert n == REDO

            def rank_in(g):
                dve.tensor_reduce(crowded[:], cand[:, :, :, 7], AX.XY, ALU.max).then_inc(s_crowd, 1)
                dve.wait_ge(s_crowd_mm, g + 1)
                dve.tensor_copy(crowded_i[:], crowd_ps).then_inc(s_crowd_i, 1)
                hold(dve, s_crowd_i, g + 1)
                any_crowded = dve.value_load(crowded_i[0:1, 0:1], min_val=0, max_val=P * N)
                with dve.If(any_crowded > 0):
                    extract_again(g)
                with dve.Else():
                    dve.sem_inc(s_redo, REDO)
                dve.tensor_scalar(found[:], top[:], 0.0, None, ALU.is_gt).then_inc(s_deg, 1)
                dve.wait_ge(s_deg, 3 * g + 1)
                dve.tensor_reduce(deg[:], found[:], AX.X, ALU.add).then_inc(s_deg, 1)
                dve.wait_ge(s_deg, 3 * g + 2)
                dve.tensor_scalar(top[:, :, S], deg[:], float(DCAP), None, ALU.min).then_inc(s_deg, 1)
                dve.wait_ge(s_deg, 3 * g + 3)
                d = top[:, :, S:S + 1].to_broadcast([P, TG, NC])
                c = class_deg[:].unsqueeze(1).to_broadcast([P, TG, NC])
                dve.tensor_tensor(inclass[:], d, c, ALU.is_equal).then_inc(s_class, 1)
                dve.tensor_tensor(above[:], d, c, ALU.is_gt).then_inc(s_class, 1)
                dve.wait_ge(s_class, 3 * g + 2)
                with nc.allow_low_precision(reason="counts up to TG"):
                    dve.tensor_reduce(above_sum[:], above[:].rearrange("p t c -> p c t"), AX.X,
                                      ALU.add).then_inc(s_class, 1)

            def rank_out(g):
                dve.wait_ge(s_rank_mm, g + 1)
                dve.tensor_tensor(picked[:], inclass[:], place_ps, ALU.mult).then_inc(s_pos, 1)
                dve.wait_ge(s_pos, 2 * g + 1)
                dve.tensor_reduce(pos[:], picked[:], AX.X, ALU.add).then_inc(s_pos, 1)
                dve.wait_ge(s_pos, 2 * g + 2)
                for t in range(TG):
                    ins = dve.tensor_scalar(to_sorted[:, t, :], column_of[:], pos[:, t:t + 1], None, ALU.is_equal)
                ins.then_inc(s_perm, 1)

            def write_lists(g, late):
                a, e = (PARTA, TG) if late else (0, PARTA)
                n = 3 * (2 * g + late)
                dve.wait_ge(s_list_mm, g + 1)
                dve.tensor_scalar(missing[:, a:e, :], list_ps[:, a:e, 0:S], 0.0, SKIP, ALU.is_equal, ALU.mult).then_inc(s_list, 1)
                dve.wait_ge(s_list, n + 1)
                dve.scalar_tensor_tensor(out=minus[:, a:e, :], in0=list_ps[:, a:e, 0:S], scalar=-1.0,
                                         in1=missing[:, a:e, :], op0=ALU.mult, op1=ALU.add).then_inc(s_list, 1)
                dve.tensor_scalar(floor[:, a:e], list_ps[:, a:e, S], float(S), LOWEST, ALU.is_gt, ALU.mult)
                dve.tensor_copy(lists[:, a:e, S], list_ps[:, a:e, S])
                dve.wait_ge(s_list, n + 2)
                dve.tensor_scalar(lists[:, a:e, 0:S], minus[:, a:e, :], table_end[:, bass.ds(g, 1)], None,
                                  ALU.add).then_inc(s_list, 1)

            def max_of(t, classes, degree):
                if len(classes) == 1:
                    dve.tensor_reduce(agg[:, t % 2, :], nbr[t % NGB][:, 0:classes[0], :].rearrange("p s c -> p c s"),
                                      AX.X, ALU.max).then_inc(s_max, 1)
                    return
                m = len(classes) // 2
                with dve.If(degree > classes[m - 1]):
                    max_of(t, classes[m:], degree)
                with dve.Else():
                    max_of(t, classes[:m], degree)

            def reduce(g, t):
                u = g * TG + t
                if t == 0:
                    dve.wait_ge(s_posrow, NH * (g + 1))
                wait(dve, s_back_mm, u - 1)
                dve.tensor_scalar(from_sorted[:, t % 2, :], posrow[:], place_of[:, t:t + 1], None,
                                  ALU.is_equal).then_inc(s_back, 1)
                degree = dve.value_load(lists[0:1, t, S:S + 1], min_val=0, max_val=DCAP)
                hold(dve, s_gather[t % NGB], 16 * MAIN * (g * (TG // NGB) + t // NGB + 1))
                max_of(t, CLASSES, degree)
                hold(dve, s_max, u + 1)
                a = agg[:, t % 2, :]
                with dve.If(degree > MAIN):
                    o = over[t > 0]
                    dve.wait_ge(s_skip[t > 0], 16 * OVF * (g * (TG - 1) + t if t else g + 1))
                    dve.tensor_reduce(agg_over[:], o[:].rearrange("p s c -> p c s"), AX.X, ALU.max).then_inc(s_over, 1)
                    dve.wait_ge(s_over, 3 * u + 1)
                    dve.tensor_tensor(a, a, agg_over[:], ALU.max).then_inc(s_over, 1)
                    dve.memset(o[:], 0.0).then_inc(s_over, 1)
                    hold(dve, s_over, 3 * u + 3)
                with dve.Else():
                    dve.sem_inc(s_over, 3)
                hi, mid, lo = (part[:, t % 2, q, :] for q in range(3))
                dve.tensor_scalar(hi, a, floor[:, t:t + 1], None, ALU.max).then_inc(s_part, 1)
                dve.wait_ge(s_part, 4 * u + 1)
                dve.scalar_tensor_tensor(out=resid[:], in0=a, scalar=floor[:, t:t + 1], in1=hi,
                                         op0=ALU.max, op1=ALU.subtract).then_inc(s_part, 1)
                dve.wait_ge(s_part, 4 * u + 2)
                dve.tensor_copy(mid, resid[:]).then_inc(s_part, 1)
                dve.wait_ge(s_part, 4 * u + 3)
                dve.tensor_tensor(lo, resid[:], mid, ALU.subtract).then_inc(s_part, 1)

            def final(g, t):
                u = g * TG + t
                dve.wait_ge(s_x[t // HB], 16 * (g + 1))
                dve.wait_ge(s_y_mm, u + 1)
                dve.scalar_tensor_tensor(out=z[:, t % 2, :], in0=ps_y[:, 0:OUT], scalar=0.0,
                                         in1=x_sb[t // HB][:, t % HB, :], op0=ALU.max, op1=ALU.add).then_inc(s_z, 1)
                dve.wait_ge(s_z, u + 1)
                dve.bn_stats(stats[:], z[:, t % 2, :]).then_inc(s_stats, 1)
                hold(dve, s_stats, u + 1)
                dve.bn_aggr(meanvar[:, t % 2, :], stats[:]).then_inc(s_mv, 1)

            def normalise(g, t):
                u = g * TG + t
                dve.wait_ge(s_sd, u + 2)
                dve.reciprocal(rstd[:], sd[:, t % 2, :]).then_inc(s_rstd, 1)
                if t % HB == 0:
                    wait(dve, s_store[t // HB], 16 * g)
                dve.wait_ge(s_rstd, u + 1)
                dve.tensor_scalar(y_sb[t // HB][:, t % HB, :], z[:, t % 2, :], meanvar[:, t % 2, 0:1], rstd[:],
                                  ALU.subtract, ALU.mult).then_inc(s_y, 1)

            def body(k):
                for i in range(TG):
                    for stage, lag in ((normalise, FLAG + 1), (reduce, RLAG), (final, FLAG), (extract, 0)):
                        g, t = lagged(k, i, lag)
                        if live(g):
                            stage(g, t)
                        if stage is normalise and i == 2 and live(k - 1):
                            wait(dve, s_pos_mm, NH * (k - 1))
                            dve.tensor_tensor(posdiag[:], ident[:].unsqueeze(1).to_broadcast([P, TG, P]),
                                              pos[:].unsqueeze(2).to_broadcast([P, TG, P]), ALU.mult).then_inc(s_diag, 1)
                    if i == 2 and live(k - 1):
                        write_lists(k - 1, 1)
                if live(k):
                    rank_in(k)
                    rank_out(k)
                    write_lists(k, 0)

            run(dve, body)


_INS = ["x", "adj", "L0_gnn_W", "L0_gnn_b"]


def kernel(**inputs):
    import numpy as _np
    import concourse.bacc as _bacc
    from concourse import mybir as _mybir
    from concourse.bass_utils import run_bass_kernel_spmd as _run

    nc = _bacc.Bacc("TRN2", target_bir_lowering=False, num_devices=1)
    arrays, args = {}, []
    for name in _INS:
        a = _np.ascontiguousarray(inputs[name])
        arrays[f"in_{name}"] = a
        args.append(nc.dram_tensor(f"in_{name}", a.shape, _mybir.dt.from_np(a.dtype), kind="ExternalInput").ap())
    out = nc.dram_tensor("out", inputs["x"].shape, F32, kind="ExternalOutput").ap()
    build(nc, *args, out)
    r = _run(nc, [arrays], core_ids=[0])
    return r.results[0]["out"]
```

```python
from contextlib import ExitStack

import concourse.bass as bass
from concourse import mybir

F32 = mybir.dt.float32
F16 = mybir.dt.float16
BF16 = mybir.dt.bfloat16
I32 = mybir.dt.int32
U32 = mybir.dt.uint32
ALU = mybir.AluOpType
ACT = mybir.ActivationFunctionType
AX = mybir.AxisListType

P = 128
S = 25
TOP = 32
NZ = 4
ROUNDS = 3
FAST = 8 * ROUNDS
CH = 256
TG = 8
G = TG * P
HB = TG // 2
RLAG = TG + 3
FLAG = 2 * TG + 3
NGB = 4
NMB = 2
MAIN = 12
OVF = S - MAIN
BASE = 4
DCAP = S + 1
NC = DCAP + 1
SKIP = float(1 << 20)
LOWEST = -3.4028235e38
EPS = 1e-5
COUNTS = list(range(4, MAIN + 1))


def build(nc, x, adj, W, b, out):
    NB, N, C = x.shape
    OUT = W.shape[1]
    NG = NB * N // G
    NCH = N // CH
    KC = C // P
    assert N == 2048 and N % G == 0 and C == OUT == 256 and G % 512 == 0 and NG > 4

    adj_v = adj.rearrange("b n m -> (b n) m").rearrange("(g p t) m -> g t p m", p=P, t=TG)
    x_rows = x.rearrange("b n c -> (b n) c")
    x_v = x_rows.rearrange("(g p h t) c -> g h p t c", p=P, h=2, t=HB)
    out_v = out.rearrange("b n c -> (b n) c").rearrange("(g p h t) c -> g h p t c", p=P, h=2, t=HB)
    W_v = W.rearrange("(k p) n -> p k n", p=P)

    with ExitStack() as ctx:
        def sb(name, shape, dt):
            return ctx.enter_context(nc.sbuf_tensor(name, shape, dt))

        def psum(name, shape, dt):
            return ctx.enter_context(nc.psum_tensor(name, shape, dt))

        def sem(name):
            return ctx.enter_context(nc.semaphore(name))

        score_of = sb("score_of", [P, N], F16)
        column_of = sb("column_of", [P, G], F16)
        place_of = sb("place_of", [P, TG], F32)
        class_deg = sb("class_deg", [P, NC], F16)
        table_end = sb("table_end", [P, NG], F32)
        ones = sb("ones", [P, P], F16)
        ident = sb("ident", [P, P], F16)
        before = sb("before", [P, P], F16)
        onesf = sb("onesf", [P, P], F32)
        identf = sb("identf", [P, P], F32)
        zeros = sb("zeros", [P, 1], F32)
        eps = sb("eps", [P, 1], F32)
        w_sb = sb("w_sb", [P, 2 * KC, OUT], F32)
        b_sb = sb("b_sb", [1, OUT], F32)
        adj_sb = sb("adj_sb", [P, NMB, N], I32)
        mask = sb("mask", [P, NMB, N], F16)
        score = sb("score", [P, TG, N], F16)
        cand = sb("cand", [P, TG, NCH, 8], F16)
        rest = sb("rest", [P, 2, NCH * 8], F16)
        top = sb("top", [P, TG, TOP], F16)
        crowded = sb("crowded", [P, TG + 1], F16)
        crowded_i = sb("crowded_i", [1, TG + 1], I32)
        found = sb("found", [P, TG, TOP], F16)
        deg = sb("deg", [P, TG], F32)
        inclass = sb("inclass", [P, TG, NC], F16)
        above = sb("above", [P, TG, NC], F16)
        above_sum = sb("above_sum", [P, NC], F16)
        picked = sb("picked", [P, TG, NC], F32)
        pos = sb("pos", [P, TG], F32)
        to_sorted = sb("to_sorted", [P, TG, G], F16)
        missing = sb("missing", [P, TG, S], F32)
        minus = sb("minus", [P, TG, S], F32)
        lists = sb("lists", [P, TG, S + 1], I32)
        floor = sb("floor", [P, TG], F32)
        posdiag = sb("posdiag", [P, TG, P], F16)
        posrow = sb("posrow", [P, G], F16)
        from_sorted = sb("from_sorted", [P, 2, G], F32)
        nbr = [sb(f"nbr{i}", [P, MAIN, C], F32) for i in range(NGB)]
        over = [sb(f"over{i}", [P, OVF, C], F32) for i in range(2)]
        agg = sb("agg", [P, 2, C], F32)
        agg_over = sb("agg_over", [P, C], F32)
        aggT = sb("aggT", [P, KC, G], F32)
        x_sb = [sb(f"x_sb{h}", [P, HB, C], F32) for h in range(2)]
        xT = sb("xT", [P, KC, P], F32)
        stats = sb("stats", [P, 6], F32)
        meanvar = sb("meanvar", [P, NZ, 2], F32)
        sd = sb("sd", [P, NZ, 1], F32)
        rstd = sb("rstd", [P, NZ, 1], F32)
        shift = sb("shift", [P, NZ, 1], F32)
        y_sb = [sb(f"y_sb{h}", [P, HB, OUT], F32) for h in range(2)]

        ps_agg = psum("ps_agg", [P, KC, G], F32)
        ps_y = psum("ps_y", [P, 512], F32)
        ps_xT = psum("ps_xT", [P, 512], F32)
        ps_rank = psum("ps_rank", [P, 512], F32)
        ps_pos = psum("ps_pos", [P, 512], F32)
        xT_ps = ps_xT[:, 0:C].rearrange("p (k m) -> p k m", k=KC)
        crowd_ps = ps_pos[0:1, 0:TG + 1]
        place_ps = ps_rank[:, 0:TG * NC].rearrange("p (t c) -> p t c", t=TG)
        list_ps = ps_rank[:, 0:TG * (S + 1)].rearrange("p (t s) -> p t s", t=TG)

        s_const = sem("s_const")
        s_ident = sem("s_ident")
        s_w = sem("s_w")
        s_adj = [sem(f"s_adj{i}") for i in range(NMB)]
        s_x = [sem(f"s_x{h}") for h in range(2)]
        s_store = [sem(f"s_store{h}") for h in range(2)]
        s_mask = sem("s_mask")
        s_zero = sem("s_zero")
        s_aggT = sem("s_aggT")
        s_xT = sem("s_xT")
        s_sd = sem("s_sd")
        s_posrow = sem("s_posrow")
        s_score = sem("s_score")
        s_cand = sem("s_cand")
        s_top = sem("s_top")
        s_rest = sem("s_rest")
        s_crowd = sem("s_crowd")
        s_crowd_i = sem("s_crowd_i")
        s_redo = sem("s_redo")
        s_deg = sem("s_deg")
        s_class = sem("s_class")
        s_pos = sem("s_pos")
        s_perm = sem("s_perm")
        s_list = sem("s_list")
        s_diag = sem("s_diag")
        s_back = sem("s_back")
        s_max = sem("s_max")
        s_over = sem("s_over")
        s_agg = sem("s_agg")
        s_z = sem("s_z")
        s_stats = sem("s_stats")
        s_mv = sem("s_mv")
        s_rstd = sem("s_rstd")
        s_y = sem("s_y")
        s_crowd_mm = sem("s_crowd_mm")
        s_rank_mm = sem("s_rank_mm")
        s_list_mm = sem("s_list_mm")
        s_pos_mm = sem("s_pos_mm")
        s_back_mm = sem("s_back_mm")
        s_xT_mm = sem("s_xT_mm")
        s_y_mm = sem("s_y_mm")
        s_gather = [sem(f"s_gather{i}") for i in range(NGB)]
        s_over_in = [sem(f"s_over_in{i}") for i in range(2)]
        NH = G // 512
        REDO = 2 * (TOP // 8) - 1
        PARTA = TG - 3

        def wait(eng, s, value):
            if not isinstance(value, int) or value > 0:
                eng.wait_ge(s, value)

        def hold(eng, s, value):
            if not isinstance(value, int):
                value = eng.to_reg(value)
            eng.wait_ge(s_const, 2)
            wait(eng, s, value)

        def live(g):
            return not isinstance(g, int) or 0 <= g < NG

        def lagged(k, i, lag):
            d, t = divmod(i - lag, TG)
            return k + d, t

        def run(eng, body):
            for k in range(3):
                body(k)
            with eng.Fori(3, NG) as k:
                body(k)
            for k in range(NG, NG + 3):
                body(k)

        block = ctx.enter_context(nc.Block())

        @block.sync
        def _(sp):
            sp.dma_start(w_sb[:], W_v).then_inc(s_w, 16)
            sp.dma_start(b_sb[:], b.rearrange("(a n) -> a n", a=1)).then_inc(s_w, 16)

            def load_adj(g):
                for t in range(TG):
                    wait(sp, s_mask, g * TG + t + 1 - NMB)
                    sp.dma_start(adj_sb[:, t % NMB, :], adj_v[g, t]).then_inc(s_adj[t % NMB], 16)

            load_adj(0)
            with sp.Fori(1, NG) as g:
                load_adj(g)

        @block.gpsimd
        def _(pool):
            pool.iota(score_of[:], [[-1, N]], base=N, channel_multiplier=0,
                      allow_small_or_imprecise_dtypes=True)
            pool.iota(column_of[:], [[1, G]], base=0, channel_multiplier=0,
                      allow_small_or_imprecise_dtypes=True)
            pool.iota(place_of[:], [[P, TG]], base=0, channel_multiplier=1,
                      allow_small_or_imprecise_dtypes=True)
            pool.iota(class_deg[:], [[-1, NC]], base=DCAP, channel_multiplier=0,
                      allow_small_or_imprecise_dtypes=True)
            pool.iota(table_end[:], [[N, NB], [0, NG // NB]], base=N, channel_multiplier=0,
                      allow_small_or_imprecise_dtypes=True)
            pool.memset(zeros[:], 0.0)
            pool.memset(eps[:], EPS)
            pool.memset(onesf[:], 1.0)
            pool.memset(over[0][:], 0.0)
            pool.memset(over[1][:], 0.0)
            pool.memset(ones[:], 1.0).then_inc(s_const, 1)
            pool.wait_ge(s_const, 1)
            pool.affine_select(out=ident[:], in_=ones[:], compare_op=ALU.is_equal, fill=0.0, base=0,
                               pattern=[[-1, P]], channel_multiplier=1)
            pool.affine_select(out=before[:], in_=ones[:], compare_op=ALU.is_gt, fill=0.0, base=0,
                               pattern=[[1, P]], channel_multiplier=-1).then_inc(s_const, 1)

            def gather(dst, t, slot, s):
                pool.indirect_dma_start(
                    out=dst, out_offset=None, in_=x_rows,
                    in_offset=bass.IndirectOffsetOnAxis(ap=lists[:, t, slot:slot + 1], axis=0),
                    bounds_check=NB * N - 1, oob_is_err=False).then_inc(s, 16)

            def main_slots(t, slot, degree):
                if slot == MAIN:
                    return
                with pool.If(degree > slot):
                    gather(nbr[t % NGB][:, slot, :], t, slot, s_gather[t % NGB])
                    main_slots(t, slot + 1, degree)
                with pool.Else():
                    pool.inc_swdge_sem([s_gather[t % NGB]], [16 * (MAIN - slot)])

            def over_slots(t, slot, degree):
                o = over[t > 0]
                s = s_over_in[t > 0]
                end = slot + 4 if slot + 8 <= S else S
                for j in range(slot, end):
                    gather(o[:, j - MAIN, :], t, j, s)
                if end < S:
                    with pool.If(degree > end):
                        over_slots(t, end, degree)
                    with pool.Else():
                        pool.inc_swdge_sem([s], [16 * (S - end)])

            def gathers(g):
                for t in range(TG):
                    if t in (0, PARTA):
                        hold(pool, s_list, 3 * (2 * g + 1 + (t >= PARTA)))
                    degree = pool.value_load(lists[0:1, t, S:S + 1], min_val=0, max_val=DCAP)
                    hold(pool, s_zero, g * TG + t + 1)
                    for slot in range(BASE):
                        gather(nbr[t % NGB][:, slot, :], t, slot, s_gather[t % NGB])
                    main_slots(t, BASE, degree)
                    with pool.If(degree > MAIN):
                        if t == 0:
                            hold(pool, s_over, 3 * ((g - 1) * TG + 1))
                        elif t == 1:
                            hold(pool, s_over, 3 * g * TG)
                        else:
                            hold(pool, s_over, 3 * (g * TG + t))
                        over_slots(t, MAIN, degree)
                        if t:
                            hold(pool, s_over_in[1], 16 * OVF * (g * (TG - 1) + t))
                    with pool.Else():
                        pool.inc_swdge_sem([s_over_in[t > 0]], [16 * OVF])

            gathers(0)
            with pool.Fori(1, NG) as g:
                gathers(g)

        @block.scalar
        def _(act):
            act.wait_ge(s_const, 1)
            act.activation(sd[:, 0, :], eps[:], ACT.Sqrt).then_inc(s_sd, 1)

            def load_x(g, h, used):
                wait(act, s_z, used)
                act.dma_start(x_sb[h][:], x_v[g, h]).then_inc(s_x[h], 16)

            def store_y(g, h):
                act.wait_ge(s_y, g * TG + HB * (h + 1))
                act.dma_start(out_v[g, h], y_sb[h][:]).then_inc(s_store[h], 16)

            def make_mask(g, t):
                u = g * TG + t
                act.wait_ge(s_adj[t % NMB], 16 * (g * (TG // NMB) + t // NMB + 1))
                wait(act, s_score, u + 1 - NMB)
                act.activation(mask[:, t % NMB, :], adj_sb[:, t % NMB, :].bitcast(U32),
                               ACT.Sign).then_inc(s_mask, 1)

            def copy_posrow(g):
                for n in range(NH):
                    act.wait_ge(s_pos_mm, g * NH + n + 1)
                    if n == 0:
                        wait(act, s_back, g * TG)
                    act.activation(posrow[:, n * 512:(n + 1) * 512], ps_pos[:], ACT.Copy).then_inc(s_posrow, 1)

            def copy_aggT(g):
                act.wait_ge(s_back_mm, (g + 1) * TG)
                wait(act, s_y_mm, g * TG)
                for c in range(KC):
                    act.activation(aggT[:, c, :], ps_agg[:, c, :], ACT.Copy).then_inc(s_aggT, 1)

            def copy_xT(g, t):
                u = g * TG + t
                act.wait_ge(s_xT_mm, u + 1)
                wait(act, s_y_mm, u)
                act.activation(xT[:], xT_ps, ACT.Copy).then_inc(s_xT, 1)

            def clear(g, t):
                wait(act, s_max, g * TG + t + 1 - NGB)
                act.activation(nbr[t % NGB][:], zeros[:].unsqueeze(2).to_broadcast([P, MAIN, C]),
                               ACT.Copy).then_inc(s_zero, 1)

            def deviation(g, t):
                act.wait_ge(s_mv, g * TG + t + 1)
                act.activation(sd[:, t % NZ, :], meanvar[:, t % NZ, 1:2], ACT.Sqrt,
                               bias=eps[:]).then_inc(s_sd, 1)

            def normalise(g, t):
                u = g * TG + t
                act.wait_ge(s_rstd, 2 * (u + 1))
                act.activation(y_sb[t // HB][:, t % HB, :], y_sb[t // HB][:, t % HB, :], ACT.Identity,
                               bias=shift[:, t % NZ, :], scale=rstd[:, t % NZ, :]).then_inc(s_y, 1)

            def body(k):
                for i in range(TG):
                    if live(k):
                        make_mask(k, i)
                    if i == 0 and live(k - 2):
                        load_x(k - 2, 0, (k - 3) * TG + HB)
                    if i == 4 and live(k - 2):
                        load_x(k - 2, 1, (k - 2) * TG)
                    if i == 3:
                        if live(k - 2):
                            copy_aggT(k - 2)
                        if live(k - 1):
                            copy_posrow(k - 1)
                    if i in (2, 6) and live(k - 3):
                        store_y(k - 3, i // 6)
                    for stage, lag in ((copy_xT, FLAG), (deviation, FLAG + 2), (normalise, FLAG + 3),
                                       (clear, RLAG - NGB)):
                        g, t = lagged(k, i, lag)
                        if live(g):
                            stage(g, t)

            act.wait_ge(s_sd, 1)
            run(act, body)
            for h in range(2):
                act.wait_ge(s_store[h], 16 * NG)

        @block.tensor
        def _(pe):
            pe.wait_ge(s_const, 2)
            pe.wait_ge(s_ident, 1)
            pe.wait_ge(s_w, 32)

            def crowd(g):
                pe.wait_ge(s_crowd, 3 * (g + 1))
                wait(pe, s_posrow, NH * g)
                pe.matmul(crowd_ps, ones[:, 0:1], crowded[:], start=True, stop=True).then_inc(s_crowd_mm, 1)

            def rank(g):
                pe.wait_ge(s_class, 3 * (g + 1))
                wait(pe, s_list, 3 * 2 * g)
                for t in range(TG):
                    pe.matmul(place_ps[:, t, :], before[:], inclass[:, t, :], start=True, stop=False)
                    for e in range(t):
                        pe.matmul(place_ps[:, t, :], ones[:], inclass[:, e, :], start=False, stop=False)
                    mm = pe.matmul(place_ps[:, t, :], ones[:], above_sum[:], start=False, stop=True)
                mm.then_inc(s_rank_mm, 1)

            def sort_lists(g):
                pe.wait_ge(s_perm, g + 1)
                for o in range(TG):
                    for t in range(TG):
                        mm = pe.matmul(list_ps[:, o, :], to_sorted[:, t, o * P:(o + 1) * P],
                                       top[:, t, 0:S + 1], start=(t == 0), stop=(t == TG - 1))
                mm.then_inc(s_list_mm, 1)

            def pos_rows(g, n):
                pe.wait_ge(s_diag, g + 1)
                wait(pe, s_posrow, g * NH + n)
                pe.matmul(ps_pos[:], ones[:], posdiag[:, 4 * n:4 * n + 4, :],
                          start=True, stop=True).then_inc(s_pos_mm, 1)

            def bring_back(g, t):
                u = g * TG + t
                if t == 0:
                    wait(pe, s_aggT, KC * g)
                pe.wait_ge(s_agg, u + 1)
                pe.wait_ge(s_back, u + 1)
                for c in range(KC):
                    for n in range(NH):
                        mm = pe.matmul(ps_agg[:, c, n * 512:(n + 1) * 512], agg[:, t % 2, c * P:(c + 1) * P],
                                       from_sorted[:, t % 2, n * 512:(n + 1) * 512],
                                       start=(t == 0), stop=(t == TG - 1))
                mm.then_inc(s_back_mm, 1)

            def linear(g, t):
                u = g * TG + t
                wait(pe, s_z, u)
                y = ps_y[:, 0:OUT]
                pe.matmul(y, onesf[0:1, :], b_sb[:], start=True, stop=False)
                if t == 0:
                    pe.wait_ge(s_aggT, KC * (g + 1))
                for c in range(KC):
                    pe.matmul(y, aggT[:, c, t * P:(t + 1) * P], w_sb[:, KC + c, :], start=False, stop=False)
                pe.wait_ge(s_xT, u + 1)
                for c in range(KC):
                    mm = pe.matmul(y, xT[:, c, :], w_sb[:, c, :], start=False, stop=(c == KC - 1))
                mm.then_inc(s_y_mm, 1)

            def transpose_x(g, t):
                pe.wait_ge(s_x[t // HB], 16 * (g + 1))
                wait(pe, s_xT, g * TG + t)
                for c in range(KC):
                    mm = pe.transpose(xT_ps[:, c, :], x_sb[t // HB][:, t % HB, c * P:(c + 1) * P], identf[:])
                mm.then_inc(s_xT_mm, 1)

            def body(k):
                for i in range(TG):
                    if i == 0 and live(k - 1):
                        rank(k - 1)
                        sort_lists(k - 1)
                    if i == 3 and live(k - 1):
                        for n in range(1, NH):
                            pos_rows(k - 1, n)
                    for stage, lag in ((bring_back, RLAG), (linear, FLAG), (transpose_x, FLAG - 1)):
                        g, t = lagged(k, i, lag)
                        if live(g):
                            stage(g, t)
                    if i == 2 and live(k - 1):
                        pe.wait_ge(s_crowd_i, k)
                        pos_rows(k - 1, 0)
                if live(k):
                    crowd(k)

            run(pe, body)

        @block.vector
        def _(dve):
            dve.wait_ge(s_const, 2)
            dve.tensor_copy(identf[:], ident[:]).then_inc(s_ident, 1)

            def scores(g, t):
                u = g * TG + t
                dve.wait_ge(s_mask, u + 1)
                dve.tensor_tensor(score[:, t, :], mask[:, t % NMB, :], score_of[:], ALU.mult).then_inc(s_score, 1)

            def chunk(g, t, c):
                u = g * TG + t
                if c == 0:
                    hold(dve, s_score, u + 1)
                ins = dve.max(cand[:, t, c, :], score[:, t, c * CH:(c + 1) * CH])
                if c == NCH - 1:
                    ins.then_inc(s_cand, 1)

            def top_step(g, t, n):
                u = g * TG + t
                r = n // 2
                src = rest[:, (r - 1) % 2, :] if r else cand[:, t].rearrange("p c e -> p (c e)")
                best = top[:, t, 8 * r:8 * r + 8]
                if n % 2 == 0:
                    if r == 0:
                        hold(dve, s_cand, u + 1)
                    else:
                        hold(dve, s_rest, (ROUNDS - 1) * u + r)
                    dve.max(best, src).then_inc(s_top, 1)
                else:
                    hold(dve, s_top, ROUNDS * u + r + 1)
                    dve.match_replace(rest[:, r % 2, :], best, src, 0.0).then_inc(s_rest, 1)

            def count_crowded(g):
                hold(dve, s_top, ROUNDS * (g + 1) * TG)
                dve.tensor_reduce(crowded[:, 0:TG], cand[:, :, :, 7], AX.X, ALU.max).then_inc(s_crowd, 1)
                dve.wait_ge(s_crowd, 3 * g + 1)
                dve.tensor_tensor(crowded[:, 0:TG], crowded[:, 0:TG], top[:, :, FAST - 1], ALU.max).then_inc(s_crowd, 1)
                dve.wait_ge(s_crowd, 3 * g + 2)
                dve.tensor_reduce(crowded[:, TG:TG + 1], crowded[:, 0:TG], AX.X, ALU.max).then_inc(s_crowd, 1)

            def search_again(g, t):
                src = score[:, t, :]
                n = g * TG * REDO + t * REDO
                for r in range(TOP // 8):
                    best = top[:, t, 8 * r:8 * r + 8]
                    dve.max(best, src).then_inc(s_redo, 1)
                    n = n + 1
                    hold(dve, s_redo, n)
                    if r < TOP // 8 - 1:
                        left = to_sorted[:, 2 * (r % 2):2 * (r % 2) + 2, :].rearrange("p a n -> p (a n)")
                        dve.match_replace(left, best, src, 0.0).then_inc(s_redo, 1)
                        n = n + 1
                        hold(dve, s_redo, n)
                        src = left

            def search_crowded(g):
                hold(dve, s_crowd_i, g + 1)
                any_crowded = dve.value_load(crowded_i[0:1, TG:TG + 1], min_val=0, max_val=P * N)
                with dve.If(any_crowded > 0):
                    for t in range(TG):
                        tile_crowded = dve.value_load(crowded_i[0:1, t:t + 1], min_val=0, max_val=P * N)
                        with dve.If(tile_crowded > 0):
                            search_again(g, t)
                        with dve.Else():
                            dve.sem_inc(s_redo, REDO)
                with dve.Else():
                    dve.sem_inc(s_redo, TG * REDO)

            def classes(g):
                dve.tensor_scalar(found[:], top[:], 0.0, None, ALU.is_gt).then_inc(s_deg, 1)
                dve.wait_ge(s_deg, 3 * g + 1)
                dve.tensor_reduce(deg[:], found[:], AX.X, ALU.add).then_inc(s_deg, 1)
                dve.wait_ge(s_deg, 3 * g + 2)
                dve.tensor_scalar(top[:, :, S], deg[:], float(DCAP), None, ALU.min).then_inc(s_deg, 1)
                dve.wait_ge(s_deg, 3 * g + 3)
                d = top[:, :, S:S + 1].to_broadcast([P, TG, NC])
                c = class_deg[:].unsqueeze(1).to_broadcast([P, TG, NC])
                dve.tensor_tensor(above[:], d, c, ALU.is_gt).then_inc(s_class, 1)
                dve.tensor_tensor(inclass[:], d, c, ALU.is_equal).then_inc(s_class, 1)
                dve.wait_ge(s_class, 3 * g + 2)
                with nc.allow_low_precision(reason="counts up to TG"):
                    dve.tensor_reduce(above_sum[:], above[:].rearrange("p t c -> p c t"), AX.X,
                                      ALU.add).then_inc(s_class, 1)

            def places(g):
                dve.wait_ge(s_rank_mm, g + 1)
                dve.tensor_tensor(picked[:], inclass[:], place_ps, ALU.mult).then_inc(s_pos, 1)
                dve.wait_ge(s_pos, 2 * g + 1)
                dve.tensor_reduce(pos[:], picked[:], AX.X, ALU.add).then_inc(s_pos, 1)

            def sort_onehots(g):
                dve.wait_ge(s_pos, 2 * g + 2)
                for t in range(TG):
                    ins = dve.tensor_scalar(to_sorted[:, t, :], column_of[:], pos[:, t:t + 1], None, ALU.is_equal)
                ins.then_inc(s_perm, 1)

            def write_lists(g, late):
                a, e = (PARTA, TG) if late else (0, PARTA)
                n = 3 * (2 * g + late)
                dve.wait_ge(s_list_mm, g + 1)
                dve.tensor_scalar(missing[:, a:e, :], list_ps[:, a:e, 0:S], 0.0, SKIP, ALU.is_equal, ALU.mult).then_inc(s_list, 1)
                dve.tensor_scalar(floor[:, a:e], list_ps[:, a:e, S], float(S), LOWEST, ALU.is_gt, ALU.mult)
                dve.tensor_copy(lists[:, a:e, S], list_ps[:, a:e, S])
                dve.wait_ge(s_list, n + 1)
                dve.scalar_tensor_tensor(out=minus[:, a:e, :], in0=list_ps[:, a:e, 0:S], scalar=-1.0,
                                         in1=missing[:, a:e, :], op0=ALU.mult, op1=ALU.add).then_inc(s_list, 1)
                dve.wait_ge(s_list, n + 2)
                dve.tensor_scalar(lists[:, a:e, 0:S], minus[:, a:e, :], table_end[:, bass.ds(g, 1)], None,
                                  ALU.add).then_inc(s_list, 1)

            def diagonals(g):
                wait(dve, s_pos_mm, NH * g)
                dve.tensor_tensor(posdiag[:], ident[:].unsqueeze(1).to_broadcast([P, TG, P]),
                                  pos[:].unsqueeze(2).to_broadcast([P, TG, P]), ALU.mult).then_inc(s_diag, 1)

            def back_onehots(g, t):
                if t == 0:
                    dve.wait_ge(s_posrow, NH * (g + 1))
                wait(dve, s_back_mm, g * TG + t - 1)
                dve.tensor_scalar(from_sorted[:, t % 2, :], posrow[:], place_of[:, t:t + 1], None,
                                  ALU.is_equal).then_inc(s_back, 1)

            def slots_max(out, buf, n):
                return dve.tensor_reduce(out, buf[:, 0:n, :].rearrange("p s c -> p c s"), AX.X, ALU.max)

            def main_max(t, counts, degree):
                if len(counts) == 1:
                    slots_max(agg[:, t % 2, :], nbr[t % NGB], counts[0]).then_inc(s_max, 1)
                    return
                m = len(counts) // 2
                with dve.If(degree > counts[m - 1]):
                    main_max(t, counts[m:], degree)
                with dve.Else():
                    main_max(t, counts[:m], degree)

            def over_max(g, t, n):
                u = g * TG + t
                o = over[t > 0]
                a = agg[:, t % 2, :]
                slots_max(agg_over[:], o, n).then_inc(s_over, 1)
                hold(dve, s_over, 3 * u + 1)
                dve.memset(o[:, 0:n, :], 0.0).then_inc(s_over, 1)
                dve.tensor_tensor(a, a, agg_over[:], ALU.max).then_inc(s_over, 1)
                hold(dve, s_over, 3 * u + 3)

            def tile_max(g, t, degree):
                u = g * TG + t
                hold(dve, s_back_mm, u - 1)
                hold(dve, s_gather[t % NGB], 16 * MAIN * (g * (TG // NGB) + t // NGB + 1))
                with dve.If(degree > MAIN):
                    main_max(t, [MAIN], degree)
                    hold(dve, s_over_in[t > 0], 16 * OVF * (g * (TG - 1) + t if t else g + 1))
                    hold(dve, s_max, u + 1)
                    with dve.If(degree > MAIN + 8):
                        over_max(g, t, OVF)
                    with dve.Else():
                        over_max(g, t, 8)
                with dve.Else():
                    main_max(t, COUNTS, degree)
                    dve.sem_inc(s_over, 3)

            def tile_floor(g, t):
                u = g * TG + t
                dve.wait_ge(s_max, u + 1)
                dve.tensor_scalar(agg[:, t % 2, :], agg[:, t % 2, :], floor[:, t:t + 1], None,
                                  ALU.max).then_inc(s_agg, 1)

            def residual(g, t):
                u = g * TG + t
                wait(dve, s_y, u + 1 - NZ)
                if t % HB == 0:
                    wait(dve, s_store[t // HB], 16 * g)
                dve.wait_ge(s_x[t // HB], 16 * (g + 1))
                dve.wait_ge(s_y_mm, u + 1)
                dve.scalar_tensor_tensor(out=y_sb[t // HB][:, t % HB, :], in0=ps_y[:, 0:OUT], scalar=0.0,
                                         in1=x_sb[t // HB][:, t % HB, :], op0=ALU.max, op1=ALU.add).then_inc(s_z, 1)

            def statistics(g, t):
                dve.wait_ge(s_z, g * TG + t + 1)
                dve.bn_stats(stats[:], y_sb[t // HB][:, t % HB, :]).then_inc(s_stats, 1)

            def aggregate(g, t):
                hold(dve, s_stats, g * TG + t + 1)
                dve.bn_aggr(meanvar[:, t % NZ, :], stats[:]).then_inc(s_mv, 1)

            def scale(g, t):
                dve.wait_ge(s_sd, g * TG + t + 2)
                dve.reciprocal(rstd[:, t % NZ, :], sd[:, t % NZ, :]).then_inc(s_rstd, 1)

            def shift_of(g, t):
                dve.wait_ge(s_rstd, 2 * (g * TG + t) + 1)
                dve.scalar_tensor_tensor(out=shift[:, t % NZ, :], in0=meanvar[:, t % NZ, 0:1], scalar=-1.0,
                                         in1=rstd[:, t % NZ, :], op0=ALU.mult, op1=ALU.mult).then_inc(s_rstd, 1)

            def body(k):
                for i in range(TG):
                    rg, rt = lagged(k, i, RLAG)
                    zg, zt = lagged(k, i, FLAG + 1)
                    ng, nt = lagged(k, i, FLAG + 2)
                    X, E, Z, V = live(k), live(rg), live(zg), live(ng)
                    R = i == 0 and live(k - 1)
                    B = i > 0 and X
                    if i == 2 and live(k - 1):
                        diagonals(k - 1)
                    if R:
                        dve.wait_ge(s_crowd_mm, k)
                        dve.tensor_copy(crowded_i[:], crowd_ps).then_inc(s_crowd_i, 1)
                        if E:
                            back_onehots(rg, rt)
                        search_crowded(k - 1)
                        classes(k - 1)
                    if i == 1 and X:
                        wait(dve, s_list_mm, k)
                        dve.memset(top[:, :, FAST:TOP], 0.0)
                    if X:
                        scores(k, i)
                    if E:
                        degree = dve.value_load(lists[0:1, rt, S:S + 1], min_val=0, max_val=DCAP)
                    if E and not R:
                        back_onehots(rg, rt)
                    if X:
                        chunk(k, i, 0)
                    if B:
                        top_step(k, i - 1, 0)
                    if E:
                        tile_max(rg, rt, degree)
                    if B:
                        top_step(k, i - 1, 1)
                    if R:
                        places(k - 1)
                    if Z:
                        residual(zg, zt)
                    if X:
                        chunk(k, i, 1)
                    if E:
                        tile_floor(rg, rt)
                    if B:
                        top_step(k, i - 1, 2)
                    if R:
                        sort_onehots(k - 1)
                    if V:
                        scale(ng, nt)
                    if X:
                        chunk(k, i, 2)
                    if Z:
                        statistics(zg, zt)
                    if B:
                        top_step(k, i - 1, 3)
                    if X:
                        chunk(k, i, 3)
                    if V:
                        shift_of(ng, nt)
                    if Z:
                        aggregate(zg, zt)
                    if X:
                        chunk(k, i, 4)
                    if B:
                        top_step(k, i - 1, 4)
                    if X:
                        for c in range(5, NCH):
                            chunk(k, i, c)
                    if R:
                        write_lists(k - 1, 0)
                    if i == 2 and live(k - 1):
                        write_lists(k - 1, 1)
                if live(k):
                    for n in range(2 * ROUNDS - 1):
                        top_step(k, TG - 1, n)
                    count_crowded(k)

            run(dve, body)


_INS = ["x", "adj", "L0_gnn_W", "L0_gnn_b"]


def kernel(**inputs):
    import numpy as _np
    import concourse.bacc as _bacc
    from concourse import mybir as _mybir
    from concourse.bass_utils import run_bass_kernel_spmd as _run

    nc = _bacc.Bacc("TRN2", target_bir_lowering=False, num_devices=1)
    arrays, args = {}, []
    for name in _INS:
        a = _np.ascontiguousarray(inputs[name])
        arrays[f"in_{name}"] = a
        args.append(nc.dram_tensor(f"in_{name}", a.shape, _mybir.dt.from_np(a.dtype), kind="ExternalInput").ap())
    out = nc.dram_tensor("out", inputs["x"].shape, F32, kind="ExternalOutput").ap()
    build(nc, *args, out)
    r = _run(nc, [arrays], core_ids=[0])
    return r.results[0]["out"]
```

```python
from contextlib import ExitStack

import concourse.bass as bass
from concourse import mybir

F32 = mybir.dt.float32
F16 = mybir.dt.float16
I32 = mybir.dt.int32
U32 = mybir.dt.uint32
U16 = mybir.dt.uint16
U8 = mybir.dt.uint8
ALU = mybir.AluOpType
ACT = mybir.ActivationFunctionType
AX = mybir.AxisListType

P = 128
S = 25
TOP = 32
NZ = 4
ROUNDS = 3
FAST = 8 * ROUNDS
CH = 256
TG = 8
G = TG * P
HB = TG // 2
AHEAD = 4
RLAG = TG + AHEAD
FLAG = RLAG + TG
ORDER = [4, 0, 7, 1, 6, 2, 5, 3]
BIG = ORDER.index(0)
NGB = 4
NMB = 2
MAIN = 12
OVF = S - MAIN
BASE = 4
DCAP = S + 1
NC = DCAP + 1
LARGEST = 3.4028235e38
EPS = 1e-5
COUNTS = list(range(BASE, MAIN + 1))


def build(nc, x, adj, W, b, out):
    NB, N, C = x.shape
    OUT = W.shape[1]
    NG = NB * N // G
    NCH = N // CH
    KC = C // P
    assert N == 2048 and N % G == 0 and C == OUT == 256 and G % 512 == 0 and NG > 4

    adj_v = adj.rearrange("b n m -> (b n) m").rearrange("(g p t) m -> g t p m", p=P, t=TG)
    x_rows = x.rearrange("b n c -> (b n) c")
    x_v = x_rows.rearrange("(g p h t) c -> g h p t c", p=P, h=2, t=HB)
    out_v = out.rearrange("b n c -> (b n) c").rearrange("(g p h t) c -> g h p t c", p=P, h=2, t=HB)
    W_v = W.rearrange("(k p) n -> p k n", p=P)

    with ExitStack() as ctx:
        def sb(name, shape, dt):
            return ctx.enter_context(nc.sbuf_tensor(name, shape, dt))

        def psum(name, shape, dt):
            return ctx.enter_context(nc.psum_tensor(name, shape, dt))

        def sem(name):
            return ctx.enter_context(nc.semaphore(name))

        score_of = sb("score_of", [P, N], F16)
        chunk_base = sb("chunk_base", [P, NCH, 8], F16)
        column_of = sb("column_of", [P, G], F16)
        minus_place = sb("minus_place", [P, TG], F32)
        class_deg = sb("class_deg", [P, NC], F16)
        table_end = sb("table_end", [P, NG], F32)
        ones = sb("ones", [P, P], F16)
        ident = sb("ident", [P, P], F16)
        before = sb("before", [P, P], F16)
        onesf = sb("onesf", [P, P], F32)
        identf = sb("identf", [P, P], F32)
        eps = sb("eps", [P, 1], F32)
        w_sb = sb("w_sb", [P, 2 * KC, OUT], F32)
        b_sb = sb("b_sb", [1, OUT], F32)
        adj_sb = sb("adj_sb", [P, NMB, N], I32)
        code = sb("code", [P, TG, N], U16)
        code_bytes = code[:].bitcast(U8).rearrange("p t (n two) -> p t n two", two=2)
        first = sb("first", [P, 2, NCH, 8], F16)
        chunk_of = sb("chunk_of", [P, 2, NCH, 8], F16)
        cand = sb("cand", [P, TG, NCH, 8], F16)
        rest = sb("rest", [P, 2, NCH * 8], F16)
        top = sb("top", [P, TG, TOP], F16)
        total = sb("total", [P, TG], F32)
        count = sb("count", [P, TG], F32)
        whole = sb("whole", [P, N], F16)
        crowded = sb("crowded", [P, TG + 1], F16)
        crowded_i = sb("crowded_i", [1, TG + 1], I32)
        found = sb("found", [P, TG, FAST], F16)
        deg = sb("deg", [P, TG], F16)
        inclass = sb("inclass", [P, TG, NC], F16)
        above = sb("above", [P, TG, NC], F16)
        above_sum = sb("above_sum", [P, NC], F16)
        picked = sb("picked", [P, TG, NC], F32)
        pos = sb("pos", [P, TG], F32)
        to_sorted = sb("to_sorted", [P, TG, G], F16)
        nearest = sb("nearest", [P, TG, 1], F32)
        spare = sb("spare", [P, TG, S], F32)
        full = sb("full", [P, TG, S], F32)
        lists = sb("lists", [P, TG, S + 1], I32)
        floor = sb("floor", [P, TG], F32)
        ceiling = sb("ceiling", [P, TG], F32)
        posdiag = sb("posdiag", [P, TG, P], F16)
        posrow = sb("posrow", [P, G], F16)
        distance = sb("distance", [P, G], F16)
        from_sorted = sb("from_sorted", [P, 2, G], F32)
        nbr = [sb(f"nbr{i}", [P, MAIN, C], F32) for i in range(NGB)]
        over = [sb(f"over{i}", [P, OVF, C], F32) for i in range(2)]
        agg = sb("agg", [P, 2, C], F32)
        agg_over = sb("agg_over", [P, C], F32)
        aggT = sb("aggT", [P, KC, G], F32)
        x_sb = [sb(f"x_sb{h}", [P, HB, C], F32) for h in range(2)]
        xT = sb("xT", [P, 2, KC, P], F32)
        stats = sb("stats", [P, 6], F32)
        meanvar = sb("meanvar", [P, NZ, 2], F32)
        sd = sb("sd", [P, NZ, 1], F32)
        rstd = sb("rstd", [P, NZ, 1], F32)
        shift = sb("shift", [P, NZ, 1], F32)
        y_sb = [sb(f"y_sb{h}", [P, HB, OUT], F32) for h in range(2)]

        ps_agg = psum("ps_agg", [P, KC, G], F32)
        ps_y = psum("ps_y", [P, 512], F32)
        ps_xT = psum("ps_xT", [P, 512], F32)
        ps_rank = psum("ps_rank", [P, 512], F32)
        ps_pos = psum("ps_pos", [P, 512], F32)
        xT_ps = ps_xT[:, 0:C].rearrange("p (k m) -> p k m", k=KC)
        crowd_ps = ps_pos[0:1, 0:TG + 1]
        place_ps = ps_rank[:, 0:TG * NC].rearrange("p (t c) -> p t c", t=TG)
        list_ps = ps_rank[:, 0:TG * (S + 1)].rearrange("p (t s) -> p t s", t=TG)

        s_const = sem("s_const")
        s_ident = sem("s_ident")
        s_w = sem("s_w")
        s_adj = [sem(f"s_adj{i}") for i in range(NMB)]
        s_x = [sem(f"s_x{h}") for h in range(2)]
        s_store = [sem(f"s_store{h}") for h in range(2)]
        s_blank = sem("s_blank")
        s_mask = sem("s_mask")
        s_aggT = sem("s_aggT")
        s_xT = sem("s_xT")
        s_sd = sem("s_sd")
        s_posrow = sem("s_posrow")
        s_first = sem("s_first")
        s_chunk = sem("s_chunk")
        s_cand = sem("s_cand")
        s_top = sem("s_top")
        s_rest = sem("s_rest")
        s_crowd = sem("s_crowd")
        s_crowd_i = sem("s_crowd_i")
        s_redo = sem("s_redo")
        s_deg = sem("s_deg")
        s_top_deg = sem("s_top_deg")
        s_class = sem("s_class")
        s_pos = sem("s_pos")
        s_perm = sem("s_perm")
        s_list = sem("s_list")
        s_diag = sem("s_diag")
        s_distance = sem("s_distance")
        s_back = sem("s_back")
        s_max = sem("s_max")
        s_over = sem("s_over")
        s_agg = sem("s_agg")
        s_z = sem("s_z")
        s_stats = sem("s_stats")
        s_mv = sem("s_mv")
        s_rstd = sem("s_rstd")
        s_y = sem("s_y")
        s_crowd_mm = sem("s_crowd_mm")
        s_rank_mm = sem("s_rank_mm")
        s_list_mm = sem("s_list_mm")
        s_pos_mm = sem("s_pos_mm")
        s_back_mm = sem("s_back_mm")
        s_xT_mm = sem("s_xT_mm")
        s_y_mm = sem("s_y_mm")
        s_gather = [sem(f"s_gather{i}") for i in range(NGB)]
        s_over_in = [sem(f"s_over_in{i}") for i in range(2)]
        NH = G // 512
        REDO = 2 * (TOP // 8)
        PARTS = {0: (0, TG - AHEAD + 1), AHEAD - 1: (TG - AHEAD + 1, TG)}
        FIRST = [a for a, _ in PARTS.values()]
        BODIES = (TG - 1 + FLAG + 4) // TG

        def others(t):
            return t - (t > BIG)

        def wait(eng, s, value):
            if not isinstance(value, int) or value > 0:
                eng.wait_ge(s, value)

        def hold(eng, s, value):
            if not isinstance(value, int):
                value = eng.to_reg(value)
            eng.wait_ge(s_const, 2)
            wait(eng, s, value)

        def live(g):
            return not isinstance(g, int) or 0 <= g < NG

        def lagged(k, i, lag):
            d, t = divmod(i - lag, TG)
            return k + d, t

        def run(eng, body):
            for k in range(BODIES):
                body(k)
            with eng.Fori(BODIES, NG) as k:
                body(k)
            for k in range(NG, NG + BODIES):
                body(k)

        def due(k, i, step):
            d, at = divmod(step, TG)
            return k - d if i == at and live(k - d) else None

        block = ctx.enter_context(nc.Block())

        @block.sync
        def _(sp):
            def load_adj(g):
                for t in range(TG):
                    wait(sp, s_mask, g * TG + t + 1 - NMB)
                    sp.dma_start(adj_sb[:, t % NMB, :], adj_v[g, t]).then_inc(s_adj[t % NMB], 16)

            load_adj(0)
            sp.dma_start(w_sb[:], W_v).then_inc(s_w, 16)
            sp.dma_start(b_sb[:], b.rearrange("(a n) -> a n", a=1)).then_inc(s_w, 16)
            with sp.Fori(1, NG) as g:
                load_adj(g)

        @block.gpsimd
        def _(pool):
            def blank(t):
                pool.iota(code[:, t, :], [[0, NCH], [-1, CH]], base=CH - 1, channel_multiplier=0,
                          allow_small_or_imprecise_dtypes=True).then_inc(s_blank, 1)

            pool.memset(eps[:], EPS)
            pool.memset(ones[:], 1.0).then_inc(s_const, 1)
            pool.wait_ge(s_const, 1)
            pool.affine_select(out=ident[:], in_=ones[:], compare_op=ALU.is_equal, fill=0.0, base=0,
                               pattern=[[-1, P]], channel_multiplier=1).then_inc(s_const, 1)
            blank(0)
            blank(1)
            pool.iota(chunk_base[:], [[-CH, NCH], [0, 8]], base=N - CH, channel_multiplier=0,
                      allow_small_or_imprecise_dtypes=True)
            pool.iota(class_deg[:], [[-1, NC]], base=DCAP, channel_multiplier=0,
                      allow_small_or_imprecise_dtypes=True)
            pool.iota(table_end[:], [[N, NB], [0, NG // NB]], base=N, channel_multiplier=0,
                      allow_small_or_imprecise_dtypes=True)
            pool.affine_select(out=before[:], in_=ones[:], compare_op=ALU.is_gt, fill=0.0, base=0,
                               pattern=[[1, P]], channel_multiplier=-1).then_inc(s_const, 1)
            for t in range(2, TG):
                blank(t)
            pool.iota(column_of[:], [[1, G]], base=0, channel_multiplier=0,
                      allow_small_or_imprecise_dtypes=True)
            for t, o in enumerate(ORDER):
                ins = pool.iota(minus_place[:, t:t + 1], [[0, 1]], base=-o * P, channel_multiplier=-1,
                                allow_small_or_imprecise_dtypes=True)
            ins.then_inc(s_const, 1)
            pool.iota(score_of[:], [[-1, N]], base=N, channel_multiplier=0,
                      allow_small_or_imprecise_dtypes=True)
            pool.memset(onesf[:], 1.0).then_inc(s_const, 1)

            def gather(dst, t, slot, s):
                pool.indirect_dma_start(
                    out=dst, out_offset=None, in_=x_rows,
                    in_offset=bass.IndirectOffsetOnAxis(ap=lists[:, t, slot:slot + 1], axis=0),
                    bounds_check=NB * N - 1, oob_is_err=False).then_inc(s, 16)

            def main_slots(t, slot, degree):
                if slot == MAIN:
                    return
                with pool.If(degree > slot):
                    gather(nbr[t % NGB][:, slot, :], t, slot, s_gather[t % NGB])
                    main_slots(t, slot + 1, degree)
                with pool.Else():
                    pool.inc_swdge_sem([s_gather[t % NGB]], [16 * (MAIN - slot)])

            def over_slots(t, slot, degree):
                o = over[t != BIG]
                s = s_over_in[t != BIG]
                gather(o[:, slot - MAIN, :], t, slot, s)
                if slot + 1 < S:
                    with pool.If(degree > slot + 1):
                        over_slots(t, slot + 1, degree)
                    with pool.Else():
                        pool.inc_swdge_sem([s], [16 * (S - slot - 1)])

            def gathers(g):
                for t in range(TG):
                    if t in FIRST:
                        hold(pool, s_list, 4 * (len(PARTS) * g + FIRST.index(t) + 1))
                    degree = pool.value_load(lists[0:1, t, S:S + 1], min_val=0, max_val=DCAP)
                    if not isinstance(g, int) or g * TG + t >= NGB:
                        hold(pool, s_max, g * TG + t + 1 - NGB)
                    for slot in range(BASE):
                        gather(nbr[t % NGB][:, slot, :], t, slot, s_gather[t % NGB])
                    main_slots(t, BASE, degree)
                    with pool.If(degree > MAIN):
                        if t == BIG:
                            hold(pool, s_over, 2 * ((g - 1) * TG + t + 1))
                        elif t > 0:
                            hold(pool, s_over, 2 * (g * TG + t - (t - 1 == BIG)))
                        else:
                            hold(pool, s_over, 2 * g * TG)
                        over_slots(t, MAIN, degree)
                        if t != BIG:
                            hold(pool, s_over_in[1], 16 * OVF * (g * (TG - 1) + others(t) + 1))
                    with pool.Else():
                        pool.inc_swdge_sem([s_over_in[t != BIG]], [16 * OVF])

            gathers(0)
            with pool.Fori(1, NG) as g:
                gathers(g)

        @block.scalar
        def _(act):
            act.wait_ge(s_const, 1)
            act.activation(sd[:, 0, :], eps[:], ACT.Sqrt).then_inc(s_sd, 1)

            def load_x(g, h, used):
                wait(act, s_z, used)
                act.dma_start(x_sb[h][:], x_v[g, h]).then_inc(s_x[h], 16)

            def store_y(g, h):
                act.wait_ge(s_y, g * TG + HB * (h + 1))
                act.dma_start(out_v[g, h], y_sb[h][:]).then_inc(s_store[h], 16)

            def make_mask(g, t):
                u = g * TG + t
                act.wait_ge(s_adj[t % NMB], 16 * (g * (TG // NMB) + t // NMB + 1))
                if isinstance(g, int) and g == 0:
                    act.wait_ge(s_blank, t + 1)
                wait(act, s_redo, REDO * (g * TG + t + 1 - TG))
                act.activation(code_bytes[:, t, :, 1], adj_sb[:, t % NMB, :].bitcast(U32),
                               ACT.Sign, accum_out=total[:, t:t + 1]).then_inc(s_mask, 1)

            def copy_posrow(g):
                for n in range(NH):
                    act.wait_ge(s_pos_mm, g * NH + n + 1)
                    if n == 0:
                        wait(act, s_back, g * TG)
                    act.activation(posrow[:, n * 512:(n + 1) * 512], ps_pos[:], ACT.Copy).then_inc(s_posrow, 1)

            def back_onehots(g, t):
                u = g * TG + t
                if isinstance(g, int) and g == 0 and t == 0:
                    act.wait_ge(s_const, 4)
                if t == 0:
                    act.wait_ge(s_posrow, NH * (g + 1))
                wait(act, s_back, u)
                act.activation(distance[:], posrow[:], ACT.Abs, bias=minus_place[:, t:t + 1]).then_inc(s_distance, 1)
                wait(act, s_back_mm, u - 1)
                act.wait_ge(s_distance, u + 1)
                act.activation(from_sorted[:, t % 2, :], distance[:], ACT.Relu, bias=1.0,
                               scale=-1.0).then_inc(s_back, 1)

            def copy_aggT(g):
                act.wait_ge(s_back_mm, (g + 1) * TG)
                wait(act, s_y_mm, g * TG)
                for c in range(KC):
                    act.activation(aggT[:, c, :], ps_agg[:, c, :], ACT.Copy).then_inc(s_aggT, 1)

            def copy_xT(g, t):
                u = g * TG + t
                act.wait_ge(s_xT_mm, u + 1)
                wait(act, s_y_mm, u - 1)
                act.activation(xT[:, t % 2], xT_ps, ACT.Copy).then_inc(s_xT, 1)

            def deviation(g, t):
                act.wait_ge(s_mv, g * TG + t + 1)
                act.activation(sd[:, t % NZ, :], meanvar[:, t % NZ, 1:2], ACT.Sqrt,
                               bias=eps[:]).then_inc(s_sd, 1)

            def normalise(g, t):
                u = g * TG + t
                act.wait_ge(s_rstd, 2 * (u + 1))
                act.activation(y_sb[t // HB][:, t % HB, :], y_sb[t // HB][:, t % HB, :], ACT.Identity,
                               bias=shift[:, t % NZ, :], scale=rstd[:, t % NZ, :]).then_inc(s_y, 1)

            def body(k):
                for i in range(TG):
                    for stage, lag in ((copy_xT, FLAG), (deviation, FLAG + 2), (normalise, FLAG + 3),
                                       (back_onehots, RLAG)):
                        g, t = lagged(k, i, lag)
                        if live(g):
                            stage(g, t)
                    g = due(k, i, RLAG - 1)
                    if g is not None:
                        copy_posrow(g)
                    if live(k) and i < TG - 1:
                        make_mask(k, i + 1 if i else 0)
                    g = due(k, i, FLAG)
                    if g is not None:
                        copy_aggT(g)
                    for h in range(2):
                        g = due(k, i, FLAG - 3 + h * HB)
                        if g is not None:
                            load_x(g, h, (g - 1) * TG + (h + 1) * HB)
                        g = due(k, i, FLAG + 3 + (h + 1) * HB)
                        if g is not None:
                            store_y(g, h)
                    if i == 0 and live(k):
                        make_mask(k, 1)

            act.wait_ge(s_sd, 1)
            run(act, body)
            for h in range(2):
                act.wait_ge(s_store[h], 16 * NG)

        @block.tensor
        def _(pe):
            pe.wait_ge(s_const, 3)
            pe.wait_ge(s_ident, 1)

            def crowd(g):
                pe.wait_ge(s_crowd, 4 * (g + 1))
                wait(pe, s_posrow, NH * g)
                pe.matmul(crowd_ps, ones[:, 0:1], crowded[:], start=True, stop=True).then_inc(s_crowd_mm, 1)

            def rank(g):
                pe.wait_ge(s_class, 3 * (g + 1))
                wait(pe, s_list, 4 * len(PARTS) * g)
                for t in range(TG):
                    pe.matmul(place_ps[:, t, :], before[:], inclass[:, t, :], start=True, stop=False)
                    for e in range(t):
                        pe.matmul(place_ps[:, t, :], ones[:], inclass[:, e, :], start=False, stop=False)
                    mm = pe.matmul(place_ps[:, t, :], ones[:], above_sum[:], start=False, stop=True)
                mm.then_inc(s_rank_mm, 1)

            def sort_lists(g):
                pe.wait_ge(s_perm, g + 1)
                pe.wait_ge(s_top_deg, g + 1)
                for o in range(TG):
                    for t in range(TG):
                        mm = pe.matmul(list_ps[:, o, :], to_sorted[:, t, ORDER[o] * P:(ORDER[o] + 1) * P],
                                       top[:, t, 0:S + 1], start=(t == 0), stop=(t == TG - 1))
                mm.then_inc(s_list_mm, 1)

            def pos_rows(g, n):
                pe.wait_ge(s_diag, g + 1)
                wait(pe, s_posrow, g * NH + n)
                pe.matmul(ps_pos[:], ones[:], posdiag[:, 4 * n:4 * n + 4, :],
                          start=True, stop=True).then_inc(s_pos_mm, 1)

            def bring_back(g, t):
                u = g * TG + t
                if t == 0:
                    wait(pe, s_aggT, KC * g)
                pe.wait_ge(s_agg, u + 1)
                pe.wait_ge(s_back, u + 1)
                for c in range(KC):
                    for n in range(NH):
                        mm = pe.matmul(ps_agg[:, c, n * 512:(n + 1) * 512], agg[:, t % 2, c * P:(c + 1) * P],
                                       from_sorted[:, t % 2, n * 512:(n + 1) * 512],
                                       start=(t == 0), stop=(t == TG - 1))
                mm.then_inc(s_back_mm, 1)

            def linear(g, t):
                u = g * TG + t
                wait(pe, s_z, u)
                y = ps_y[:, 0:OUT]
                if isinstance(g, int) and g == 0 and t == 0:
                    pe.wait_ge(s_const, 5)
                    pe.wait_ge(s_w, 32)
                pe.matmul(y, onesf[0:1, :], b_sb[:], start=True, stop=False)
                if t == 0:
                    pe.wait_ge(s_aggT, KC * (g + 1))
                for c in range(KC):
                    pe.matmul(y, aggT[:, c, t * P:(t + 1) * P], w_sb[:, KC + c, :], start=False, stop=False)
                pe.wait_ge(s_xT, u + 1)
                for c in range(KC):
                    mm = pe.matmul(y, xT[:, t % 2, c, :], w_sb[:, c, :], start=False, stop=(c == KC - 1))
                mm.then_inc(s_y_mm, 1)

            def transpose_x(g, t):
                pe.wait_ge(s_x[t // HB], 16 * (g + 1))
                wait(pe, s_xT, g * TG + t)
                for c in range(KC):
                    mm = pe.transpose(xT_ps[:, c, :], x_sb[t // HB][:, t % HB, c * P:(c + 1) * P], identf[:])
                mm.then_inc(s_xT_mm, 1)

            def body(k):
                for i in range(TG):
                    if i == 0 and live(k - 1):
                        sort_lists(k - 1)
                    g = due(k, i, RLAG - 1)
                    if g is not None:
                        pe.wait_ge(s_crowd_i, g + 1)
                        for n in range(NH):
                            pos_rows(g, n)
                    for stage, lag in ((transpose_x, FLAG - 1), (linear, FLAG), (bring_back, RLAG)):
                        if i == TG - 1 and stage is linear and live(k):
                            rank(k)
                        g, t = lagged(k, i, lag)
                        if live(g):
                            stage(g, t)
                    if i == TG - 1 and live(k):
                        crowd(k)

            run(pe, body)

        @block.vector
        def _(dve):
            dve.wait_ge(s_const, 2)
            dve.tensor_copy(identf[:], ident[:]).then_inc(s_ident, 1)

            def chunk(g, t, c):
                u = g * TG + t
                if c == 0:
                    hold(dve, s_mask, u + 1)
                ins = dve.max(first[:, t % 2, c, :], code[:, t, c * CH:(c + 1) * CH])
                if c == NCH - 1:
                    ins.then_inc(s_first, 1)

            def candidates(g, t, n):
                u = g * TG + t
                if n == 0:
                    dve.wait_ge(s_first, u + 1)
                    dve.scalar_tensor_tensor(out=chunk_of[:, t % 2], in0=first[:, t % 2], scalar=float(CH),
                                             in1=chunk_base[:], op0=ALU.is_ge, op1=ALU.mult).then_inc(s_chunk, 1)
                else:
                    dve.wait_ge(s_chunk, u + 1)
                    dve.scalar_tensor_tensor(out=cand[:, t], in0=first[:, t % 2], scalar=float(1 - CH),
                                             in1=chunk_of[:, t % 2], op0=ALU.add, op1=ALU.add).then_inc(s_cand, 1)

            def top_step(g, t, n):
                u = g * TG + t
                r = n // 2
                src = rest[:, (r - 1) % 2, :] if r else cand[:, t].rearrange("p c e -> p (c e)")
                best = top[:, t, 8 * r:8 * r + 8]
                if n % 2 == 0:
                    if r == 0:
                        hold(dve, s_cand, u + 1)
                    else:
                        hold(dve, s_rest, (ROUNDS - 1) * u + r)
                    dve.max(best, src).then_inc(s_top, 1)
                else:
                    hold(dve, s_top, ROUNDS * u + r + 1)
                    dve.match_replace(rest[:, r % 2, :], best, src, 0.0).then_inc(s_rest, 1)

            def count_crowded(g, n):
                if n == 0:
                    dve.wait_ge(s_top, ROUNDS * (g + 1) * TG)
                    dve.tensor_scalar(found[:], top[:, :, 0:FAST], 0.0, None, ALU.is_gt).then_inc(s_crowd, 1)
                elif n == 1:
                    dve.wait_ge(s_crowd, 4 * g + 1)
                    dve.tensor_reduce(count[:], found[:], AX.X, ALU.add).then_inc(s_crowd, 1)
                elif n == 2:
                    dve.wait_ge(s_crowd, 4 * g + 2)
                    dve.tensor_tensor(crowded[:, 0:TG], total[:], count[:], ALU.subtract).then_inc(s_crowd, 1)
                else:
                    dve.wait_ge(s_crowd, 4 * g + 3)
                    dve.tensor_reduce(crowded[:, TG:TG + 1], crowded[:, 0:TG], AX.X, ALU.max).then_inc(s_crowd, 1)

            def search_again(g, t):
                n = g * TG * REDO + t * REDO
                dve.scalar_tensor_tensor(out=whole[:], in0=code[:, t, :], scalar=float(CH), in1=score_of[:],
                                         op0=ALU.is_ge, op1=ALU.mult).then_inc(s_redo, 1)
                n = n + 1
                hold(dve, s_redo, n)
                for r in range(TOP // 8):
                    best = top[:, t, 8 * r:8 * r + 8]
                    dve.max(best, whole[:]).then_inc(s_redo, 1)
                    n = n + 1
                    hold(dve, s_redo, n)
                    if r < TOP // 8 - 1:
                        dve.match_replace(whole[:], best, whole[:], 0.0).then_inc(s_redo, 1)
                        n = n + 1
                        hold(dve, s_redo, n)

            def search_crowded(g):
                if isinstance(g, int) and g == 0:
                    dve.wait_ge(s_const, 5)
                hold(dve, s_crowd_i, g + 1)
                any_crowded = dve.value_load(crowded_i[0:1, TG:TG + 1], min_val=0, max_val=P * N)
                with dve.If(any_crowded > 0):
                    for t in range(TG):
                        tile_crowded = dve.value_load(crowded_i[0:1, t:t + 1], min_val=0, max_val=P * N)
                        with dve.If(tile_crowded > 0):
                            search_again(g, t)
                        with dve.Else():
                            dve.sem_inc(s_redo, REDO)
                with dve.Else():
                    dve.sem_inc(s_redo, TG * REDO)

            def cap_degrees(g):
                dve.wait_ge(s_mask, (g + 1) * TG)
                dve.tensor_scalar(deg[:], total[:], float(DCAP), None, ALU.min).then_inc(s_deg, 1)

            def classes(g, n):
                if n == 0:
                    dve.wait_ge(s_deg, g + 1)
                    d = deg[:].unsqueeze(2).to_broadcast([P, TG, NC])
                    c = class_deg[:].unsqueeze(1).to_broadcast([P, TG, NC])
                    dve.tensor_tensor(above[:], d, c, ALU.is_gt).then_inc(s_class, 1)
                    dve.tensor_tensor(inclass[:], d, c, ALU.is_equal).then_inc(s_class, 1)
                else:
                    dve.wait_ge(s_class, 3 * g + 2)
                    with nc.allow_low_precision(reason="counts up to TG"):
                        dve.tensor_reduce(above_sum[:], above[:].rearrange("p t c -> p c t"), AX.X,
                                          ALU.add).then_inc(s_class, 1)

            def file_degrees(g):
                dve.wait_ge(s_redo, REDO * (g + 1) * TG)
                dve.tensor_copy(top[:, :, S], deg[:]).then_inc(s_top_deg, 1)

            def places(g, n):
                if n == 0:
                    if isinstance(g, int) and g == 0:
                        dve.wait_ge(s_const, 4)
                    dve.wait_ge(s_rank_mm, g + 1)
                    dve.tensor_tensor(picked[:], inclass[:], place_ps, ALU.mult).then_inc(s_pos, 1)
                else:
                    dve.wait_ge(s_pos, 2 * g + 1)
                    dve.tensor_reduce(pos[:], picked[:], AX.X, ALU.add).then_inc(s_pos, 1)

            def sort_onehots(g):
                dve.wait_ge(s_pos, 2 * g + 2)
                for t in range(TG):
                    ins = dve.tensor_scalar(to_sorted[:, t, :], column_of[:], pos[:, t:t + 1], None, ALU.is_equal)
                ins.then_inc(s_perm, 1)

            def write_lists(g, a, e):
                n = 4 * (len(PARTS) * g + FIRST.index(a))
                dve.wait_ge(s_list_mm, g + 1)
                dve.tensor_scalar(nearest[:, a:e, :], list_ps[:, a:e, 0:1], 1.0, None, ALU.max).then_inc(s_list, 1)
                wait(dve, s_agg, (g - 1) * TG + e)
                dve.tensor_scalar(floor[:, a:e], list_ps[:, a:e, S], float(S), -LARGEST, ALU.is_gt, ALU.mult)
                dve.tensor_scalar(ceiling[:, a:e], list_ps[:, a:e, S], 0.0, LARGEST, ALU.is_gt, ALU.mult)
                dve.tensor_copy(lists[:, a:e, S], list_ps[:, a:e, S])
                dve.wait_ge(s_list, n + 1)
                dve.scalar_tensor_tensor(out=spare[:, a:e, :], in0=list_ps[:, a:e, 0:S], scalar=0.0,
                                         in1=nearest[:, a:e, :].to_broadcast([P, e - a, S]), op0=ALU.is_le,
                                         op1=ALU.mult).then_inc(s_list, 1)
                dve.wait_ge(s_list, n + 2)
                dve.scalar_tensor_tensor(out=full[:, a:e, :], in0=list_ps[:, a:e, 0:S], scalar=0.0,
                                         in1=spare[:, a:e, :], op0=ALU.max, op1=ALU.add).then_inc(s_list, 1)
                dve.wait_ge(s_list, n + 3)
                dve.tensor_scalar(lists[:, a:e, 0:S], full[:, a:e, :], -1.0, table_end[:, bass.ds(g, 1)],
                                  ALU.mult, ALU.add).then_inc(s_list, 1)

            def diagonals(g):
                wait(dve, s_pos_mm, NH * g)
                dve.tensor_tensor(posdiag[:], ident[:].unsqueeze(1).to_broadcast([P, TG, P]),
                                  pos[:].unsqueeze(2).to_broadcast([P, TG, P]), ALU.mult).then_inc(s_diag, 1)

            def slots_max(out, buf, n):
                return dve.tensor_reduce(out, buf[:, 0:n, :].rearrange("p s c -> p c s"), AX.X, ALU.max)

            def load_degree(g, t):
                return dve.value_load(lists[0:1, t, S:S + 1], min_val=0, max_val=DCAP)

            def main_max(g, t, counts, degree):
                if len(counts) == 1:
                    dve.wait_ge(s_gather[t % NGB], 16 * MAIN * (g * (TG // NGB) + t // NGB + 1))
                    slots_max(agg[:, t % 2, :], nbr[t % NGB], counts[0]).then_inc(s_max, 1)
                    return
                m = len(counts) // 2
                with dve.If(degree > counts[m - 1]):
                    main_max(g, t, counts[m:], degree)
                with dve.Else():
                    main_max(g, t, counts[:m], degree)

            def over_max(g, t, counts, degree):
                if len(counts) == 1:
                    slots_max(agg_over[:], over[t != BIG], counts[0]).then_inc(s_over, 1)
                    return
                m = len(counts) // 2
                with dve.If(degree > MAIN + counts[m - 1]):
                    over_max(g, t, counts[m:], degree)
                with dve.Else():
                    over_max(g, t, counts[:m], degree)

            def tile_max(g, t, degree):
                u = g * TG + t
                hold(dve, s_back_mm, u - 1)
                with dve.If(degree > MAIN):
                    main_max(g, t, [MAIN], degree)
                    hold(dve, s_over_in[t != BIG], 16 * OVF * (g + 1 if t == BIG else g * (TG - 1) + others(t) + 1))
                    over_max(g, t, list(range(1, OVF + 1)), degree)
                    dve.wait_ge(s_max, u + 1)
                    dve.wait_ge(s_over, 2 * u + 1)
                    a = agg[:, t % 2, :]
                    dve.tensor_tensor(a, a, agg_over[:], ALU.max).then_inc(s_over, 1)
                with dve.Else():
                    main_max(g, t, COUNTS, degree)
                    dve.sem_inc(s_over, 2)

            def tile_floor(g, t):
                u = g * TG + t
                dve.wait_ge(s_max, u + 1)
                dve.wait_ge(s_over, 2 * (u + 1))
                dve.tensor_scalar(agg[:, t % 2, :], agg[:, t % 2, :], floor[:, t:t + 1], ceiling[:, t:t + 1],
                                  ALU.max, ALU.min).then_inc(s_agg, 1)

            def residual(g, t):
                u = g * TG + t
                wait(dve, s_y, u + 1 - NZ)
                if t % HB == 0:
                    wait(dve, s_store[t // HB], 16 * g)
                dve.wait_ge(s_x[t // HB], 16 * (g + 1))
                dve.wait_ge(s_y_mm, u + 1)
                dve.scalar_tensor_tensor(out=y_sb[t // HB][:, t % HB, :], in0=ps_y[:, 0:OUT], scalar=0.0,
                                         in1=x_sb[t // HB][:, t % HB, :], op0=ALU.max, op1=ALU.add).then_inc(s_z, 1)

            def statistics(g, t):
                dve.wait_ge(s_z, g * TG + t + 1)
                dve.bn_stats(stats[:], y_sb[t // HB][:, t % HB, :]).then_inc(s_stats, 1)

            def aggregate(g, t):
                hold(dve, s_stats, g * TG + t + 1)
                dve.bn_aggr(meanvar[:, t % NZ, :], stats[:]).then_inc(s_mv, 1)

            def scale(g, t):
                dve.wait_ge(s_sd, g * TG + t + 2)
                dve.reciprocal(rstd[:, t % NZ, :], sd[:, t % NZ, :]).then_inc(s_rstd, 1)

            def shift_of(g, t):
                dve.wait_ge(s_rstd, 2 * (g * TG + t) + 1)
                dve.scalar_tensor_tensor(out=shift[:, t % NZ, :], in0=meanvar[:, t % NZ, 0:1], scalar=-1.0,
                                         in1=rstd[:, t % NZ, :], op0=ALU.mult, op1=ALU.mult).then_inc(s_rstd, 1)

            def do(stage, step, *more):
                if live(step[0]):
                    return stage(*step, *more)


            def first_step(k):
                x, e = (k, 0), lagged(k, 0, RLAG)
                z, v = lagged(k, 0, FLAG + 1), lagged(k, 0, FLAG + 2)
                ranked = live(k - 1)
                if ranked:
                    dve.wait_ge(s_crowd_mm, k)
                    dve.tensor_copy(crowded_i[:], crowd_ps).then_inc(s_crowd_i, 1)
                if ranked:
                    search_crowded(k - 1)
                    file_degrees(k - 1)
                do(scale, v)
                degree = do(load_degree, e)
                do(residual, z)
                do(shift_of, v)
                do(tile_max, e, degree)
                do(statistics, z)
                do(tile_floor, e)
                do(chunk, x, 0)
                do(aggregate, z)
                do(chunk, x, 1)
                do(chunk, x, 2)
                if ranked:
                    write_lists(k - 1, *PARTS[0])
                for c in range(3, NCH):
                    do(chunk, x, c)
                if isinstance(k, int) and k == 0:
                    dve.wait_ge(s_const, 3)

            def middle_step(k, i):
                x, b, e = (k, i), (k, i - 1), lagged(k, i, RLAG)
                z, v = lagged(k, i, FLAG + 1), lagged(k, i, FLAG + 2)
                degree = do(load_degree, e)
                do(chunk, x, 0)
                do(candidates, b, 0)
                do(chunk, x, 1)
                do(candidates, b, 1)
                for c in range(2, 6):
                    do(chunk, x, c)
                do(tile_max, e, degree)
                if i == 1 and live(k):
                    wait(dve, s_list_mm, k)
                    dve.memset(top[:, :, FAST:S], 0.0)
                do(top_step, b, 0)
                do(residual, z)
                do(top_step, b, 1)
                do(tile_floor, e)
                do(top_step, b, 2)
                do(statistics, z)
                do(top_step, b, 3)
                do(scale, v)
                do(aggregate, z)
                do(top_step, b, 4)
                do(shift_of, v)
                for c in range(6, NCH):
                    do(chunk, x, c)
                if i in PARTS and live(k - 1):
                    write_lists(k - 1, *PARTS[i])
                g = due(k, i, RLAG - 2)
                if g is not None:
                    diagonals(g)

            def last_step(k):
                x, b, e = (k, TG - 1), (k, TG - 2), lagged(k, TG - 1, RLAG)
                z, v = lagged(k, TG - 1, FLAG + 1), lagged(k, TG - 1, FLAG + 2)
                degree = do(load_degree, e)
                do(chunk, x, 0)
                if live(k):
                    cap_degrees(k)
                do(candidates, b, 0)
                if live(k):
                    classes(k, 0)
                do(candidates, b, 1)
                if live(k):
                    classes(k, 1)
                do(residual, z)
                for c in range(1, 4):
                    do(chunk, x, c)
                do(tile_max, e, degree)
                do(top_step, b, 0)
                do(chunk, x, 4)
                do(top_step, b, 1)
                do(tile_floor, e)
                do(top_step, b, 2)
                do(chunk, x, 5)
                do(top_step, b, 3)
                do(chunk, x, 6)
                do(top_step, b, 4)
                do(chunk, x, 7)
                do(candidates, x, 0)
                do(scale, v)
                do(candidates, x, 1)
                do(statistics, z)
                do(top_step, x, 0)
                if live(k):
                    places(k, 0)
                do(top_step, x, 1)
                do(shift_of, v)
                if live(k):
                    places(k, 1)
                do(top_step, x, 2)
                do(aggregate, z)
                do(top_step, x, 3)
                if live(k):
                    sort_onehots(k)
                do(top_step, x, 4)
                for n in range(4):
                    if live(k):
                        count_crowded(k, n)

            def body(k):
                first_step(k)
                for i in range(1, TG - 1):
                    middle_step(k, i)
                last_step(k)

            run(dve, body)


_INS = ["x", "adj", "L0_gnn_W", "L0_gnn_b"]


def kernel(**inputs):
    import numpy as _np
    import concourse.bacc as _bacc
    from concourse import mybir as _mybir
    from concourse.bass_utils import run_bass_kernel_spmd as _run

    nc = _bacc.Bacc("TRN2", target_bir_lowering=False, num_devices=1)
    arrays, args = {}, []
    for name in _INS:
        a = _np.ascontiguousarray(inputs[name])
        arrays[f"in_{name}"] = a
        args.append(nc.dram_tensor(f"in_{name}", a.shape, _mybir.dt.from_np(a.dtype), kind="ExternalInput").ap())
    out = nc.dram_tensor("out", inputs["x"].shape, F32, kind="ExternalOutput").ap()
    build(nc, *args, out)
    r = _run(nc, [arrays], core_ids=[0])
    return r.results[0]["out"]
```
